# Optimizing a Trainium2 kernel written in Bass

```python
import numpy as np
import jax
import jax.numpy as jnp

def _softmax(x, axis=-1):
    return jax.nn.softmax(x, axis=axis)

def _gelu(x):
    return jax.nn.gelu(x, approximate=True)

def _silu(x):
    return jax.nn.silu(x)

def _sigmoid(x):
    return jax.nn.sigmoid(x)

def _layernorm(x, axis=-1, eps=1e-05):
    m = jnp.mean(x, axis=axis, keepdims=True)
    v = jnp.var(x, axis=axis, keepdims=True)
    return (x - m) / jnp.sqrt(v + eps)

def _scatter_add(tgt, idx, src, axis=0):
    return tgt.at[idx].add(src)

def _segment_sum(src, seg, n):
    return jax.ops.segment_sum(src, seg, n)
kernel_name = 'mk_prb_d1_jaxref_r8_f1bb26'

def setup_inputs(seed: int=0):
    np.random.seed(seed)
    _w = jnp.asarray

    def _L0_attn_setup():
        import jax, jax.numpy as jnp
        import numpy as np
        B, S, DM = (2, 256, 256)
        H, KVH, HD = (16, 4, 128)
        REP = H // KVH
        ROPE_BASE = 10000.0
        EPS = 1e-06

        def _rope_tables(seq_len, dim):
            inv_freq = 1.0 / ROPE_BASE ** (jnp.arange(0, dim, 2, dtype=jnp.float32) / dim)
            t = jnp.arange(seq_len, dtype=jnp.float32)
            freqs = jnp.outer(t, inv_freq)
            emb = jnp.concatenate([freqs, freqs], -1)
            return (jnp.cos(emb), jnp.sin(emb))

        def _rotate_half(x):
            d = x.shape[-1] // 2
            return jnp.concatenate([-x[..., d:], x[..., :d]], axis=-1)
        key = jax.random.key(seed)
        k0, k1, k2, k3, k4 = jax.random.split(key, 5)
        w = lambda k, o, i: jax.random.normal(k, (o, i), jnp.float32) * (1.0 / np.sqrt(i))
        return {'x': jax.random.normal(k0, (B, S, DM), jnp.float32), 'Wq': w(k1, H * HD, DM), 'Wk': w(k2, KVH * HD, DM), 'Wv': w(k3, KVH * HD, DM), 'Wo': w(k4, DM, H * HD)}
    _L0_attn_in = _L0_attn_setup()

    def _L0_ffn_setup():
        import jax, jax.numpy as jnp
        import numpy as np
        D_MODEL = 256
        D_EXPERT = 1024
        EPS = 1e-08

        def ternary_quant(w):
            scale = jnp.mean(jnp.abs(w)) + EPS
            q = jnp.clip(jnp.round(w / scale), -1.0, 1.0) * scale
            return w + jax.lax.stop_gradient(q - w)
        key = jax.random.key(seed)
        k_x, k_up, k_gate, k_down = jax.random.split(key, 4)
        std_in = 1.0 / np.sqrt(D_MODEL)
        std_exp = 1.0 / np.sqrt(D_EXPERT)
        return {'x': jax.random.normal(k_x, (4, 256, D_MODEL), dtype=jnp.float32), 'W_up': jax.random.normal(k_up, (D_EXPERT, D_MODEL), dtype=jnp.float32) * std_in, 'W_gate': jax.random.normal(k_gate, (D_EXPERT, D_MODEL), dtype=jnp.float32) * std_in, 'W_down': jax.random.normal(k_down, (D_MODEL, D_EXPERT), dtype=jnp.float32) * std_exp}
    _L0_ffn_in = _L0_ffn_setup()
    _d = {'L0_attn_x': _L0_attn_in['x'], 'L0_attn_Wq': _L0_attn_in['Wq'], 'L0_attn_Wk': _L0_attn_in['Wk'], 'L0_attn_Wv': _L0_attn_in['Wv'], 'L0_attn_Wo': _L0_attn_in['Wo'], 'L0_ffn_W_up': _L0_ffn_in['W_up'], 'L0_ffn_W_gate': _L0_ffn_in['W_gate'], 'L0_ffn_W_down': _L0_ffn_in['W_down']}
    _x0 = _d['L0_attn_x']
    _d['L0_attn_x'] = jax.random.normal(jax.random.fold_in(jax.random.key(seed), 1), (2, 512, 256), dtype=_x0.dtype)
    del _x0
    return _d

def reference(L0_attn_x, L0_attn_Wq, L0_attn_Wk, L0_attn_Wv, L0_attn_Wo, L0_ffn_W_up, L0_ffn_W_gate, L0_ffn_W_down):

    def _L0_attn_ref(x, Wq, Wk, Wv, Wo):
        import jax, jax.numpy as jnp
        import numpy as np
        B, S, DM = (2, 256, 256)
        H, KVH, HD = (16, 4, 128)
        REP = H // KVH
        ROPE_BASE = 10000.0
        EPS = 1e-06

        def _rope_tables(seq_len, dim):
            inv_freq = 1.0 / ROPE_BASE ** (jnp.arange(0, dim, 2, dtype=jnp.float32) / dim)
            t = jnp.arange(seq_len, dtype=jnp.float32)
            freqs = jnp.outer(t, inv_freq)
            emb = jnp.concatenate([freqs, freqs], -1)
            return (jnp.cos(emb), jnp.sin(emb))

        def _rotate_half(x):
            d = x.shape[-1] // 2
            return jnp.concatenate([-x[..., d:], x[..., :d]], axis=-1)
        bsz, seq_len, _ = x.shape
        q = (x @ Wq.T).reshape(bsz, seq_len, H, HD).transpose(0, 2, 1, 3)
        k = (x @ Wk.T).reshape(bsz, seq_len, KVH, HD).transpose(0, 2, 1, 3)
        v = (x @ Wv.T).reshape(bsz, seq_len, KVH, HD).transpose(0, 2, 1, 3)
        cos, sin = _rope_tables(seq_len, HD)
        cos, sin = (cos[None, None], sin[None, None])
        q = q * cos + _rotate_half(q) * sin
        k = k * cos + _rotate_half(k) * sin
        k = jnp.repeat(k, REP, axis=1)
        v = jnp.repeat(v, REP, axis=1)
        qf = jax.nn.elu(q) + 1.0
        kf = jax.nn.elu(k) + 1.0
        qf_t = qf.transpose(2, 0, 1, 3)
        kf_t = kf.transpose(2, 0, 1, 3)
        v_t = v.transpose(2, 0, 1, 3)

        def step(carry, inp):
            state, z = carry
            q_s, k_s, v_s = inp
            state = state + k_s[..., :, None] * v_s[..., None, :]
            z = z + k_s
            num = jnp.einsum('bhe,bhed->bhd', q_s, state)
            den = jnp.einsum('bhe,bhe->bh', q_s, z)[..., None] + EPS
            return ((state, z), num / den)
        init = (jnp.zeros((bsz, H, HD, HD), x.dtype), jnp.zeros((bsz, H, HD), x.dtype))
        _, out = jax.lax.scan(step, init, (qf_t, kf_t, v_t))
        out = out.transpose(1, 0, 2, 3).reshape(bsz, seq_len, H * HD)
        return out @ Wo.T

    def _L0_ffn_ref(x, W_up, W_gate, W_down):
        import jax, jax.numpy as jnp
        import numpy as np
        D_MODEL = 256
        D_EXPERT = 1024
        EPS = 1e-08

        def ternary_quant(w):
            scale = jnp.mean(jnp.abs(w)) + EPS
            q = jnp.clip(jnp.round(w / scale), -1.0, 1.0) * scale
            return w + jax.lax.stop_gradient(q - w)
        wu = ternary_quant(W_up)
        wg = ternary_quant(W_gate)
        wd = ternary_quant(W_down)
        up = jnp.einsum('bsd,ed->bse', x, wu)
        gate = jnp.einsum('bsd,ed->bse', x, wg)
        hidden = jax.nn.silu(up) * gate
        return jnp.einsum('bse,de->bsd', hidden, wd)
    x = L0_attn_x
    xn = _layernorm(x, axis=-1)
    x = x + _L0_attn_ref(xn, L0_attn_Wq, L0_attn_Wk, L0_attn_Wv, L0_attn_Wo) + _L0_ffn_ref(xn, L0_ffn_W_up, L0_ffn_W_gate, L0_ffn_W_down)
    return x

_drawn_inputs = setup_inputs


def setup_inputs(seed=0):
    import zlib

    import numpy as np

    out = dict(_drawn_inputs(seed))
    spreads = {}
    factors = {'L0_attn_Wq': 26.54, 'L0_attn_Wk': 20.29}
    for name, (base, spread) in spreads.items():
        noise = np.random.default_rng([zlib.crc32(name.encode()), seed]).standard_normal(out[name].shape)
        drawn = base * np.exp(spread * noise) if base else spread * noise
        out[name] = jnp.asarray(drawn.astype(out[name].dtype))
    for name, factor in factors.items():
        out[name] = (out[name] * factor).astype(out[name].dtype)
    return out
```

```python
from contextlib import ExitStack

import concourse.bass as bass
import numpy as np
from concourse import mybir

F32 = mybir.dt.float32
F32R = mybir.dt.float32r
ALU = mybir.AluOpType
ACT = mybir.ActivationFunctionType

P = 128
B, S, DM = 2, 512, 256
H, KVH, HD = 16, 4, 128
REP = H // KVH
FF = 1024
CT = DM // P
NC = S // P
TILES = B * NC
UNITS = TILES * KVH
FT = FF // P
KV = KVH * HD
LN_EPS = 1e-5
DEN_EPS = 1e-6
TERN_EPS = 1e-8

W_K = 0
W_V = W_K + CT * KV
W_Q = W_V + CT * KV
W_O = W_Q + CT * H * HD
W_ALL = W_O + H * DM
W_CHUNK = W_ALL // (B * FT)
T_UP, T_GATE, T_DOWN = 0, CT * FF, 2 * CT * FF
T_ALL = 3 * CT * FF

ROUNDS, PER_ROUND = 3, 2 * KVH
SLOTS_BEFORE = range(-KVH, 1)
SLOTS_AFTER = range(ROUNDS * PER_ROUND + 1, UNITS + 1)
SCALE_BLOCK = 1.0 / (FF * DM)


START = 1


def wait_round(engine, sem, c, per_round, count, start=0):
    if c is None:
        if count > 0:
            engine.wait_ge(sem, count + start)
    else:
        assert count + start > 0
        engine.wait_ge(sem, c * per_round + count + start)


def tile_of(slot):
    return slot // KVH


def proj_index(tile, what):
    return 6 * tile + {"k": 0, "v": 1}.get(what, 2 + what if isinstance(what, int) else 0)


def rope_index(tile, what):
    return 5 * tile + (0 if what == "k" else 1 + what)


def slot_projections(k):
    tile, g = tile_of(k), k % KVH
    order = {0: [(tile, 3), (tile + 1, "k")], 1: [(tile + 1, "v"), (tile + 1, 0)],
             2: [(tile + 1, 1)], 3: [(tile + 1, 2)]}[g]
    return [(t, w) for t, w in order if 0 <= t < TILES]


def transposes_k(k):
    return k % KVH == 2 and 0 <= tile_of(k) + 1 < TILES


def is_unit(k):
    return 0 <= k < UNITS


def has_state(tile):
    return 0 <= tile < TILES - B


def build(nc, x, w_attn, w_ffn, consts, out):
    with ExitStack() as ctx:
        def sem(name):
            return ctx.enter_context(nc.semaphore(name))

        r_words = 2 * W_ALL + 2 * CT * B * S + T_ALL + 4 * 4 * KV + 2 * 2 * CT * P + 2 * P
        f_tmp = T_ALL + 2 * W_CHUNK + 2 * 512
        f_words = TILES * DM + max(f_tmp, 17 * KV) + 2 * NC * HD + 3 * P
        region_r = ctx.enter_context(nc.sbuf_tensor("region_r", [P, r_words], F32R))
        region_f = ctx.enter_context(nc.sbuf_tensor("region_f", [P, f_words], F32))
        small = ctx.enter_context(nc.sbuf_tensor("small", [P, 160], F32))
        used = {"r": 0, "f": 0}

        def take(region, words):
            at = used[region]
            used[region] += words
            return (region_r if region == "r" else region_f)[:, at:at + words]

        w_split = take("r", 2 * W_ALL).rearrange("p (s n) -> p s n", s=2)
        xt_split = take("r", 2 * CT * B * S).rearrange("p (s c t) -> p s c t", s=2, c=CT)
        shared_r = take("r", T_ALL)
        tern = shared_r
        heads4 = shared_r.rearrange("p (w s r n) -> p w s r n", w=3, s=2, r=2)
        v_split, kt_split, k_split = heads4[:, 0], heads4[:, 1], heads4[:, 2]
        qt_split = take("r", 4 * KV).rearrange("p (s r n) -> p s r n", s=2, r=2)
        p_split = take("r", 4 * KV).rearrange("p (s r n) -> p s r n", s=2, r=2)
        hid_split = p_split
        o_split = take("r", 4 * KV).rearrange("p (s r n) -> p s r n", s=2, r=2)
        state_split = take("r", 4 * KV).rearrange("p (s r n) -> p s r n", s=2, r=2)
        x_stat = take("r", 2 * 2 * CT * P).rearrange("p (r s c t) -> p r s c t", r=2, s=2, c=CT)
        tri = take("r", P)
        ones = take("r", P)

        acc = take("f", TILES * DM).rearrange("p (t n) -> p t n", t=TILES)
        shared_f = take("f", max(f_tmp, 17 * KV))
        t_raw = shared_f[:, 0:T_ALL]
        w_raw = shared_f[:, T_ALL:T_ALL + 2 * W_CHUNK].rearrange("p (r n) -> p r n", r=2)
        hid = shared_f[:, T_ALL + 2 * W_CHUNK:f_tmp].rearrange("p (r n) -> p r n", r=2)
        xn = shared_f[:, T_ALL:T_ALL + TILES * DM].rearrange("p (t n) -> p t n", t=TILES)
        att = shared_f[:, 0:17 * KV].rearrange("p (b n) -> p b n", n=KV)
        rope_a, rope_b, q_feat = att[:, 0:2], att[:, 2:4], att[:, 4:6]
        p_mask, o_copy, z_sum = att[:, 6:8], att[:, 8:10], att[:, 10:12]
        k_total, state, k_feat = att[:, 12:14], att[:, 14:16], att[:, 16]
        const_f = take("f", 2 * NC * HD + 3 * P)
        cos_t = const_f[:, 0:NC * HD].rearrange("p (c n) -> p c n", c=NC)
        sin_t = const_f[:, NC * HD:2 * NC * HD].rearrange("p (c n) -> p c n", c=NC)
        mask = const_f[:, 2 * NC * HD:2 * NC * HD + P]
        ident = const_f[:, 2 * NC * HD + P:2 * NC * HD + 2 * P]
        ones_f = const_f[:, 2 * NC * HD + 2 * P:2 * NC * HD + 3 * P]

        stats = small[:, 0:6 * TILES].rearrange("p (t n) -> p t n", t=TILES)
        moments = small[:, 48:48 + 2 * TILES].rearrange("p (t n) -> p t n", t=TILES)
        var, root, rstd, newton = (small[:, 64 + 8 * i:72 + 8 * i] for i in range(4))
        abs_sum = small[:, 96:102]
        scale, thresh, neg_thresh = small[:, 102:105], small[:, 105:108], small[:, 108:111]
        up_scale, gd_scale = small[:, 111:112], small[:, 112:113]
        den = small[:, 120:128].rearrange("p (r h) -> p r h", r=2)
        rden = small[:, 128:136].rearrange("p (r h) -> p r h", r=2)

        bank = ctx.enter_context(nc.psum_tensor("bank", [P, 8, 512], F32))
        ps_abs = bank[:, 0:2, :]
        ps_total = [bank[:, 2 + w % 2, 0:1] for w in range(3)]
        ps_xt = bank[:, 4:8, :]
        ps_up, ps_gate, ps_ffn = bank[:, 0:2, :], bank[:, 2:4, :], bank[:, 4:8, 0:DM]
        ps_proj, ps_score = bank[:, 0:2, :], bank[:, 2:4, :]
        ps_o, ps_tr, ps_sum, ps_y = bank[:, 4, :], bank[:, 5, :], bank[:, 6, :], bank[:, 7, :]

        x_loaded = [sem(f"x_loaded{b}") for b in range(B)]
        ident_loaded, consts_loaded = sem("ident_loaded"), sem("consts_loaded")
        t_loaded = [sem(f"t_loaded{w}") for w in range(3)]
        w_loaded = [sem(f"w_loaded{r}") for r in range(2)]
        ln_step, root_done, xn_done = sem("ln_step"), sem("root_done"), sem("xn_done")
        abs_done, total_done, tern_step = sem("abs_done"), sem("total_done"), sem("tern_step")
        tern_done = sem("tern_done")
        xt_done, xt_hi, xt_ready = sem("xt_done"), sem("xt_hi"), sem("xt_ready")
        flags_done = sem("flags_done")
        gate_done, silu_done, hid_done = sem("gate_done"), sem("silu_done"), sem("hid_done")
        hid_hi, hid_ready, down_done = sem("hid_hi"), sem("hid_ready"), sem("down_done")
        ffn_added, w_hi, w_ready = sem("ffn_added"), sem("w_hi"), sem("w_ready")

        x_stat_loaded = [sem(f"x_stat_loaded{r}") for r in range(2)]
        zeroed = sem("zeroed")
        projected, proj_read = sem("projected"), sem("proj_read")
        rotated, clipped, exped = sem("rotated"), sem("clipped"), sem("exped")
        q_formed, den_done, rden_done, normed = (sem(n) for n in ("q_formed", "den_done", "rden_done", "normed"))
        k_formed, k_hi, k_ready = sem("k_formed"), sem("k_hi"), sem("k_ready")
        v_hi = sem("v_hi")
        transposed, tr_hi, tr_ready = sem("transposed"), sem("tr_hi"), sem("tr_ready")
        sum_done, sum_read = sem("sum_done"), sem("sum_read")
        scored, masked, p_hi, p_ready = sem("scored"), sem("masked"), sem("p_hi"), sem("p_ready")
        o_done, o_hi, o_copied, o_ready = sem("o_done"), sem("o_hi"), sem("o_copied"), sem("o_ready")
        state_hi, state_ready = sem("state_hi"), sem("state_ready")
        y_done, y_half, out_ready, out_stored = sem("y_done"), sem("y_half"), sem("out_ready"), sem("out_stored")

        block = ctx.enter_context(nc.Block())

        def heads(ap):
            return ap.rearrange("p (h n) -> p h n", h=REP)

        @block.sync
        def _(sp):
            x_in = x.rearrange("b (c p) n -> b p c n", p=P)
            out_v = out.rearrange("b (c p) n -> b p c n", p=P)
            n_const = 2 * NC * HD
            sp.dma_start(acc[:, 0:NC], x_in[0]).then_inc(x_loaded[0], 16)
            sp.dma_start(t_raw[:, T_UP:T_GATE], w_ffn[:, T_UP:T_GATE]).then_inc(t_loaded[0], 16)
            sp.dma_start(acc[:, NC:TILES], x_in[1]).then_inc(x_loaded[1], 16)
            sp.dma_start(const_f[:, n_const:], consts[:, n_const:]).then_inc(ident_loaded, 16)
            sp.dma_start(t_raw[:, T_GATE:T_DOWN], w_ffn[:, T_GATE:T_DOWN]).then_inc(t_loaded[1], 16)
            sp.dma_start(t_raw[:, T_DOWN:], w_ffn[:, T_DOWN:]).then_inc(t_loaded[2], 16)
            sp.dma_start(const_f[:, 0:n_const], consts[:, 0:n_const]).then_inc(consts_loaded, 16)

            sp.wait_ge(xt_done, B * CT)
            for i in range(2):
                sp.dma_start(w_raw[:, i], w_attn[:, i * W_CHUNK:(i + 1) * W_CHUNK]).then_inc(w_loaded[i], 16)
            with sp.Fori(0, B * FT // 2 - 1) as pair:
                for r in range(2):
                    sp.wait_ge(w_ready, pair * 2 + r + 1)
                    sp.dma_start(w_raw[:, r], w_attn[:, bass.ds((pair * 2 + r + 2) * W_CHUNK, W_CHUNK)]
                                 ).then_inc(w_loaded[r], 16)

            def load_x_stat(c, tile):
                r = tile % 2
                wait_round(sp, projected, c, 6 * 2, proj_index(tile - 2, 3) + 1)
                chunk = tile // B if c is None else c + tile // B
                sp.dma_start(x_stat[:, r].bitcast(F32),
                             xt_split[:, :, :, bass.ds(chunk * P + (tile % B) * S, P)].bitcast(F32)
                             ).then_inc(x_stat_loaded[r], 16)

            def store(c, tile):
                wait_round(sp, out_ready, c, 2, tile + 1, START)
                chunk = tile // B if c is None else c + tile // B
                b = tile % B
                sp.dma_start(out_v[b][:, bass.ds(chunk, 1), :],
                             acc[:, bass.ds(chunk + b * NC, 1), :]).then_inc(out_stored, 16)

            sp.wait_ge(xt_ready, B * CT)
            load_x_stat(None, 0)
            load_x_stat(None, 1)
            with sp.Fori(0, ROUNDS) as c:
                for tile in range(2):
                    load_x_stat(c, tile + 2)
                    store(c, tile)
            for tile in range(TILES - 2, TILES):
                store(None, tile)
            sp.wait_ge(out_stored, 16 * TILES)

        @block.tensor
        def _(pe):
            for counter in (down_done, sum_done, o_done, y_done):
                pe.sem_inc(counter, START)
            pe.wait_ge(ident_loaded, 16)
            for w in range(3):
                pe.wait_ge(abs_done, 2 * w + 2)
                if w == 2:
                    pe.wait_ge(tern_step, 1)
                for i in range(2):
                    mm = nc.tensor.matmul(ps_total[w], ones_f, abs_sum[:, 2 * w + i:2 * w + i + 1],
                                          start=(i == 0), stop=(i == 1))
                mm.then_inc(total_done, 1)
                if w == 0:
                    for b in range(B):
                        pe.wait_ge(xn_done, NC * (b + 1))
                        for half in range(CT):
                            for t in range(NC):
                                mm = nc.tensor.transpose(ps_xt[:, CT * b + half, t * P:(t + 1) * P],
                                                         xn[:, NC * b + t, half * P:(half + 1) * P], ident)
                            mm.then_inc(xt_done, 1)

            def down(b, j):
                pe.wait_ge(hid_ready, b * FT + j + 1 + START)
                for lo in range(2):
                    for t in range(NC):
                        mm = nc.tensor.matmul(ps_ffn[:, t], hid_split[:, lo, j % 2, t * P:(t + 1) * P],
                                              tern[:, T_DOWN + j * DM:T_DOWN + (j + 1) * DM],
                                              start=(j == 0 and lo == 0), stop=(j == FT - 1 and lo == 1))
                mm.then_inc(down_done, 1)

            pe.wait_ge(xt_ready, B * CT)
            pe.wait_ge(tern_done, 3)
            with pe.Fori(0, B) as b:
                for j in range(FT):
                    pe.wait_ge(hid_done, b * FT + max(j - 1, 0) + START)
                    for ps, at in ((ps_up, T_UP), (ps_gate, T_GATE)):
                        for half in range(CT):
                            col = at + half * FF + j * P
                            for lo in range(2):
                                mm = nc.tensor.matmul(ps[:, j % 2], tern[:, col:col + P],
                                                      xt_split[:, lo, half, bass.ds(b * S, S)],
                                                      start=(half == 0 and lo == 0),
                                                      stop=(half == CT - 1 and lo == 1))
                    mm.then_inc(gate_done, 1)
                    if j == 1:
                        pe.wait_ge(ffn_added, b + START)
                    if j:
                        down(b, j - 1)
                down(b, FT - 1)

            def project(c, tile, what):
                r = tile % 2
                n = proj_index(tile, what)
                if what == "k":
                    wait_round(pe, x_stat_loaded[r], c, 16, 16 * (tile // 2 + 1))
                wait_round(pe, proj_read, c, 12, n - 1)
                col, step = {"k": (W_K, KV), "v": (W_V, KV)}.get(what) or (W_Q + what * KV, H * HD)
                passes = [(s, w, half) for half in range(CT) for s, w in ((0, 0), (0, 1), (1, 0))]
                for i, (s, w, half) in enumerate(passes):
                    at = col + half * step
                    mm = nc.tensor.matmul(ps_proj[:, n % 2], x_stat[:, r, s, half],
                                          w_split[:, w, at:at + KV], start=(i == 0), stop=(i == len(passes) - 1))
                mm.then_inc(projected, 1)

            def transpose(c, tile, what):
                if what == "k":
                    wait_round(pe, k_formed, c, 2, tile + 1)
                    src = k_feat
                else:
                    wait_round(pe, normed, c, 8, KVH * tile + what + 1)
                    src = q_feat[:, what % 2]
                n = rope_index(tile, what)
                wait_round(pe, tr_ready, c, 10, n)
                for h in range(REP):
                    mm = nc.tensor.transpose(ps_tr[:, h * P:(h + 1) * P], src[:, h * P:(h + 1) * P], ident)
                mm.then_inc(transposed, 1)

            def slot(c, k):
                tile, g = tile_of(k), k % KVH
                r, kr = tile % 2, k % 2
                if is_unit(k):
                    wait_round(pe, tr_ready, c, 10, rope_index(tile, g) + 1)
                    wait_round(pe, masked, c, 8, k - 1, START)
                    for i, (s, m) in enumerate(((0, 0), (0, 1), (1, 0))):
                        mm = nc.tensor.matmul(ps_score[:, kr], kt_split[:, s, r, g * P:(g + 1) * P],
                                              qt_split[:, m, kr], start=(i == 0), stop=(i == 2))
                    mm.then_inc(scored, 1)
                for t, what in slot_projections(k):
                    project(c, t, what)
                if is_unit(k + 1):
                    transpose(c, tile_of(k + 1), (k + 1) % KVH)
                if is_unit(k - 1):
                    wait_round(pe, o_hi, c, 8, k)
                    tw, gw, pr = tile_of(k - 1), (k - 1) % KVH, (k - 1) % 2
                    if gw == 0:
                        wait_round(pe, out_ready, c, 2, tw, START)
                    for s in range(2):
                        if s == 1:
                            wait_round(pe, o_ready, c, 8, k, START)
                        for h in range(REP):
                            at = W_O + (gw * REP + h) * DM
                            first, last = gw == 0 and s == 0 and h == 0, gw == KVH - 1 and s == 1 and h == REP - 1
                            o_st = o_split[:, s, pr, h * P:(h + 1) * P]
                            if s == 0:
                                mm = nc.tensor.matmul(ps_y.rearrange("p (w n) -> p w n", w=2), o_st,
                                                      w_split[:, :, at:at + DM], start=first, stop=last)
                            else:
                                mm = nc.tensor.matmul(ps_y[:, 0:DM], o_st, w_split[:, 0, at:at + DM],
                                                      start=first, stop=last)
                    mm.then_inc(y_done, 1)
                if g == 0 and has_state(tile):
                    wait_round(pe, sum_read, c, 6, 3 * tile + 2, START)
                    wait_round(pe, proj_read, c, 12, proj_index(tile, "v") + 1)
                    for j in range(KVH):
                        cols = slice(j * P, (j + 1) * P)
                        for i, (s, m) in enumerate(((0, 0), (0, 1), (1, 0))):
                            mm = nc.tensor.matmul(ps_sum[:, cols], k_split[:, s, r, cols], v_split[:, m, r, cols],
                                                  start=(i == 0), stop=(i == 2))
                    mm.then_inc(sum_done, 1)
                if (g == 1 and 0 <= tile + 1 < TILES) or (g == 2 and has_state(tile + 1)):
                    new = tile + 1
                    wait_round(pe, k_ready, c, 2, new + 1)
                    wait_round(pe, sum_read, c, 6, 3 * new + g - 1, START)
                    for s in range(2):
                        mm = nc.tensor.matmul(ps_sum, tri if g == 1 else ones, k_split[:, s, new % 2],
                                              start=(s == 0), stop=(s == 1))
                    mm.then_inc(sum_done, 1)
                if transposes_k(k):
                    transpose(c, tile + 1, "k")
                if is_unit(k):
                    wait_round(pe, o_copied, c, 8, k)
                    wait_round(pe, state_ready, c, 2, tile + 1)
                    for i, (s, m) in enumerate(((0, 0), (0, 1), (1, 0))):
                        nc.tensor.matmul(ps_o, state_split[:, s, r, g * P:(g + 1) * P], qt_split[:, m, kr],
                                         start=(i == 0), stop=False)
                    wait_round(pe, proj_read, c, 12, proj_index(tile, "v") + 1)
                    wait_round(pe, p_hi, c, 8, k + 1)
                    for s in range(2):
                        nc.tensor.matmul(ps_o, v_split[:, s, r, g * P:(g + 1) * P], p_split[:, 0, kr],
                                         start=False, stop=False)
                    wait_round(pe, p_ready, c, 8, k + 1, START)
                    nc.tensor.matmul(ps_o, v_split[:, 0, r, g * P:(g + 1) * P], p_split[:, 1, kr],
                                     start=False, stop=True).then_inc(o_done, 1)

            pe.wait_ge(w_ready, B * FT)
            pe.wait_ge(flags_done, 2)
            for k in SLOTS_BEFORE:
                slot(None, k)
            with pe.Fori(0, ROUNDS) as c:
                for k in range(1, PER_ROUND + 1):
                    slot(c, k)
            for k in SLOTS_AFTER:
                slot(None, k)

        @block.vector
        def _(dve):
            v = nc.vector
            for counter in (hid_done, ffn_added, masked, sum_read, out_ready):
                dve.sem_inc(counter, START)
            step = [0]

            def chained(sem, ins):
                step[0] += 1
                ins.then_inc(sem, 1)
                dve.wait_ge(sem, step[0])

            for t in range(TILES):
                if t % NC == 0:
                    dve.wait_ge(x_loaded[t // NC], 16)
                ins = v.bn_stats(stats[:, t], acc[:, t])
            chained(ln_step, ins)
            for t in range(TILES):
                ins = v.bn_aggr(moments[:, t], stats[:, t])
            chained(ln_step, ins)
            chained(ln_step, v.tensor_scalar(var, moments[:, :, 1], LN_EPS, None, ALU.add))
            dve.wait_ge(root_done, 1)
            chained(ln_step, v.reciprocal(rstd, root))
            chained(ln_step, v.tensor_tensor(newton, rstd, rstd, ALU.mult))
            chained(ln_step, v.tensor_tensor(newton, newton, var, ALU.mult))
            chained(ln_step, v.tensor_scalar(newton, newton, -0.5, 1.5, ALU.mult, ALU.add))
            chained(ln_step, v.tensor_tensor(rstd, rstd, newton, ALU.mult))
            for t in range(TILES):
                v.tensor_scalar(xn[:, t], acc[:, t], moments[:, t, 0:1], rstd[:, t:t + 1],
                                ALU.subtract, ALU.mult).then_inc(xn_done, 1)

            step[0] = 0
            for w, at in enumerate((T_UP, T_GATE, T_DOWN)):
                cols = slice(at, at + CT * FF)
                dve.wait_ge(total_done, w + 1)
                one = slice(w, w + 1)
                chained(tern_step, v.tensor_scalar(scale[:, one], ps_total[w], SCALE_BLOCK, TERN_EPS,
                                                   ALU.mult, ALU.add))
                v.tensor_scalar(thresh[:, one], scale[:, one], 0.5, None, ALU.mult)
                chained(tern_step, v.tensor_scalar(neg_thresh[:, one], scale[:, one], -0.5, None, ALU.mult))
                chained(tern_step, v.tensor_scalar(tern[:, cols], t_raw[:, cols], thresh[:, one], None, ALU.is_gt))
                v.scalar_tensor_tensor(tern[:, cols], t_raw[:, cols], neg_thresh[:, one],
                                       tern[:, cols].bitcast(F32), ALU.is_lt, ALU.subtract).then_inc(tern_done, 1)
                if w == 0:
                    v.tensor_scalar(up_scale, scale[:, one], -1.0, None, ALU.mult)
                    for i in range(B * CT):
                        dve.wait_ge(xt_hi, i + 1)
                        dst = xt_split[:, :, i % CT, (i // CT) * S:(i // CT + 1) * S]
                        v.tensor_tensor(dst[:, 1], ps_xt[:, i], dst[:, 0].bitcast(F32), ALU.subtract
                                        ).then_inc(xt_ready, 1)
            chained(tern_step, v.tensor_tensor(gd_scale, scale[:, 1:2], scale[:, 2:3], ALU.mult))

            with dve.Fori(0, B) as b:
                for j in range(FT):
                    n = b * FT + j
                    dve.wait_ge(silu_done, n + 1)
                    v.scalar_tensor_tensor(hid[:, j % 2], ps_gate[:, j % 2], gd_scale, hid[:, j % 2],
                                           ALU.mult, ALU.mult).then_inc(hid_done, 1)
                    dve.wait_ge(w_hi, n + 1)
                    cols = bass.ds(n * W_CHUNK, W_CHUNK)
                    v.tensor_tensor(w_split[:, 1, cols], w_raw[:, j % 2], w_split[:, 0, cols].bitcast(F32),
                                    ALU.subtract).then_inc(w_ready, 1)
                dve.wait_ge(down_done, b * FT + FT + START)
                batch = acc[:, bass.ds(b * NC, NC), :]
                v.tensor_tensor(batch, ps_ffn, batch, ALU.add).then_inc(ffn_added, 1)

            dve.wait_ge(consts_loaded, 16)
            dve.wait_ge(ident_loaded, 16)
            dve.wait_ge(zeroed, 2)
            dve.wait_ge(ffn_added, B + START)

            def rotate(c, tile, what):
                n, w = proj_index(tile, what), rope_index(tile, what)
                chunk = tile // B if c is None else c + tile // B
                wait_round(dve, projected, c, 12, n + 1)
                prev = (tile, what)
                src = ps_proj[:, n % 2]
                v.tensor_tensor(heads(rope_a[:, w % 2]), heads(src),
                                cos_t[:, bass.ds(chunk, 1), :].broadcast_to([P, REP, HD]), ALU.mult)
                swapped = src.rearrange("p (h u e) -> p h u e", h=REP, u=2)[:, :, ::-1, :]
                sin = sin_t[:, bass.ds(chunk, 1), :].rearrange("p o (u e) -> p o u e", u=2)
                v.tensor_tensor(rope_b[:, w % 2].rearrange("p (h u e) -> p h u e", h=REP, u=2), swapped,
                                sin.broadcast_to([P, REP, 2, HD // 2]), ALU.mult).then_inc(proj_read, 1)

            def split_transposed(c, tile, what):
                w = rope_index(tile, what)
                wait_round(dve, tr_hi, c, 10, w + 1)
                dst = kt_split[:, :, tile % 2] if what == "k" else qt_split[:, :, what % 2]
                v.tensor_tensor(dst[:, 1], ps_tr, dst[:, 0].bitcast(F32), ALU.subtract).then_inc(tr_ready, 1)

            def slot(c, k):
                tile, g = tile_of(k), k % KVH
                new = tile + 1
                if g == 1 and 0 <= new < TILES:
                    wait_round(dve, exped, c, 10, rope_index(new, "k") + 1)
                    v.scalar_tensor_tensor(k_feat, rope_a[:, rope_index(new, "k") % 2], 1.0, k_feat,
                                           ALU.add, ALU.max).then_inc(k_formed, 1)
                f = k + 2
                if is_unit(f):
                    ft, fg, fr = tile_of(f), f % KVH, f % 2
                    w = rope_index(ft, fg)
                    wait_round(dve, exped, c, 10, w + 1)
                    v.scalar_tensor_tensor(q_feat[:, fr], rope_a[:, w % 2], 1.0, q_feat[:, fr],
                                           ALU.add, ALU.max).then_inc(q_formed, 1)
                if is_unit(k):
                    wait_round(dve, scored, c, 8, k + 1)
                    wait_round(dve, p_ready, c, 8, k - 1, START)
                    v.tensor_tensor(heads(p_mask[:, k % 2]), heads(ps_score[:, k % 2]),
                                    mask.rearrange("p (o n) -> p o n", o=1).broadcast_to([P, REP, P]),
                                    ALU.mult).then_inc(masked, 1)
                if g == 1 and 0 <= new < TILES:
                    wait_round(dve, k_hi, c, 2, new + 1)
                    v.tensor_tensor(k_split[:, 1, new % 2], k_feat, k_split[:, 0, new % 2].bitcast(F32),
                                    ALU.subtract).then_inc(k_ready, 1)
                if is_unit(f):
                    wait_round(dve, q_formed, c, 8, f + 1)
                    wait_round(dve, sum_read, c, 6, 3 * ft + 1, START)
                    wait_round(dve, normed, c, 8, f - 1)
                    for h in range(REP):
                        cols = slice(h * P, (h + 1) * P)
                        ins = v.tensor_tensor_reduce(out=rope_b[:, w % 2, cols], in0=q_feat[:, fr, cols],
                                                     in1=z_sum[:, ft % 2, fg * P:(fg + 1) * P], scale=1.0,
                                                     scalar=DEN_EPS, op0=ALU.mult, op1=ALU.add,
                                                     accum_out=den[:, fr, h:h + 1])
                    ins.then_inc(den_done, 1)
                for i, (t, what) in enumerate(slot_projections(k)):
                    if what == "v":
                        wait_round(dve, v_hi, c, 2, t + 1)
                        v.tensor_tensor(v_split[:, 1, t % 2], ps_proj[:, proj_index(t, what) % 2],
                                        v_split[:, 0, t % 2].bitcast(F32), ALU.subtract).then_inc(proj_read, 1)
                    else:
                        rotate(c, t, what)
                    if i == 0 and is_unit(f):
                        wait_round(dve, den_done, c, 8, f + 1)
                        v.reciprocal(rden[:, fr], den[:, fr]).then_inc(rden_done, 1)
                if not slot_projections(k) and is_unit(f):
                    wait_round(dve, den_done, c, 8, f + 1)
                    v.reciprocal(rden[:, fr], den[:, fr]).then_inc(rden_done, 1)
                if is_unit(k + 1):
                    split_transposed(c, tile_of(k + 1), (k + 1) % KVH)
                if g == 0 and has_state(tile):
                    wait_round(dve, sum_done, c, 6, 3 * tile + 3, START)
                    wait_round(dve, state_ready, c, 2, tile + 1)
                    v.tensor_tensor(state[:, tile % 2], ps_sum, state[:, tile % 2], ALU.add).then_inc(sum_read, 1)
                if g == 1 and 0 <= new < TILES:
                    wait_round(dve, sum_done, c, 6, 3 * new + 1, START)
                    wait_round(dve, sum_read, c, 6, 3 * new - 3, START)
                    v.tensor_tensor(z_sum[:, new % 2], ps_sum, k_total[:, new % 2], ALU.add).then_inc(sum_read, 1)
                if g == 2 and has_state(new):
                    wait_round(dve, sum_done, c, 6, 3 * new + 2, START)
                    v.tensor_tensor(k_total[:, new % 2], ps_sum, k_total[:, new % 2], ALU.add
                                    ).then_inc(sum_read, 1)
                if transposes_k(k):
                    split_transposed(c, new, "k")
                if g == 0 and has_state(tile - 1):
                    old = tile - 1
                    wait_round(dve, state_hi, c, 2, old + 1)
                    v.tensor_tensor(state_split[:, 1, old % 2], state[:, old % 2],
                                    state_split[:, 0, old % 2].bitcast(F32), ALU.subtract).then_inc(state_ready, 1)
                if g == 0 and 0 <= tile - 1 < TILES:
                    old = tile - 1
                    wait_round(dve, y_done, c, 8, KVH * old + KVH, START)
                    chunk = old // B if c is None else c + old // B
                    dst = acc[:, bass.ds(chunk + (old % B) * NC, 1), :]
                    y = ps_y.rearrange("p (w n) -> p w n", w=2)
                    v.tensor_tensor(dst, y[:, 0:1], dst, ALU.add).then_inc(y_half, 1)
                    wait_round(dve, y_half, c, 2, old + 1)
                    v.tensor_tensor(dst, y[:, 1:2], dst, ALU.add).then_inc(out_ready, 1)

            for k in SLOTS_BEFORE:
                slot(None, k)
            with dve.Fori(0, ROUNDS) as c:
                for k in range(1, PER_ROUND + 1):
                    slot(c, k)
            for k in SLOTS_AFTER:
                slot(None, k)

        @block.scalar
        def _(act):
            s = nc.scalar
            act.wait_ge(ln_step, 3)
            s.activation(root, var, ACT.Sqrt).then_inc(root_done, 1)
            for i in range(6):
                if i % 2 == 0:
                    act.wait_ge(t_loaded[i // 2], 16)
                if i:
                    act.wait_ge(abs_done, i)
                s.activation(ps_abs.rearrange("p a n -> p (a n)"), t_raw[:, i * FF:(i + 1) * FF], ACT.Abs,
                             accum_out=abs_sum[:, i:i + 1]).then_inc(abs_done, 1)
                if i == 1:
                    for n in range(B * CT):
                        act.wait_ge(xt_done, n + 1)
                        s.activation(xt_split[:, 0, n % CT, (n // CT) * S:(n // CT + 1) * S], ps_xt[:, n],
                                     ACT.Copy).then_inc(xt_hi, 1)
            act.wait_ge(ident_loaded, 16)
            s.activation(tri, mask, ACT.Copy).then_inc(flags_done, 1)
            s.activation(ones, ones_f, ACT.Copy).then_inc(flags_done, 1)
            act.wait_ge(tern_step, 7)

            with act.Fori(0, B) as b:
                for j in range(FT):
                    n = b * FT + j
                    act.wait_ge(gate_done, n + 1)
                    act.wait_ge(hid_ready, b * FT + max(j - 1, 0) + START)
                    s.activation(hid[:, j % 2], ps_up[:, j % 2], ACT.Silu, scale=up_scale).then_inc(silu_done, 1)
                    act.wait_ge(w_loaded[j % 2], (b * (FT // 2) + j // 2 + 1) * 16)
                    s.activation(w_split[:, 0, bass.ds(n * W_CHUNK, W_CHUNK)], w_raw[:, j % 2], ACT.Copy
                                 ).then_inc(w_hi, 1)
                    act.wait_ge(hid_done, n + 1 + START)
                    act.wait_ge(down_done, b * FT + max(j - 1, 0) + START)
                    s.activation(hid_split[:, 0, j % 2], hid[:, j % 2], ACT.Copy).then_inc(hid_hi, 1)

            def exp(c, tile, what):
                w = rope_index(tile, what)
                wait_round(act, rotated, c, 10, w + 1)
                if what == "k":
                    wait_round(act, transposed, c, 10, rope_index(tile - 1, "k") + 1)
                    wait_round(act, k_ready, c, 2, tile)
                    dst = k_feat
                else:
                    wait_round(act, transposed, c, 10, rope_index(*divmod(KVH * tile + what - 2, KVH)) + 1)
                    dst = q_feat[:, what % 2]
                s.activation(dst, rope_a[:, w % 2], ACT.Relu, scale=-1.0).then_inc(clipped, 1)
                wait_round(act, clipped, c, 10, w + 1)
                s.activation(dst, dst, ACT.Exp, scale=-1.0).then_inc(exped, 1)

            def split_transposed(c, tile, what):
                wait_round(act, transposed, c, 10, rope_index(tile, what) + 1)
                if what == "k":
                    wait_round(act, o_done, c, 8, KVH * (tile - 1), START)
                    dst = kt_split[:, 0, tile % 2]
                else:
                    wait_round(act, o_done, c, 8, KVH * tile + what - 1, START)
                    dst = qt_split[:, 0, what % 2]
                s.activation(dst, ps_tr, ACT.Copy).then_inc(tr_hi, 1)

            def slot(c, k):
                tile, g = tile_of(k), k % KVH
                new = tile + 1
                if is_unit(k - 1):
                    wait_round(act, o_done, c, 8, k, START)
                    wait_round(act, y_done, c, 8, k - 1, START)
                    s.activation(o_split[:, 0, (k - 1) % 2], ps_o, ACT.Copy).then_inc(o_hi, 1)
                    wait_round(act, o_ready, c, 8, k - 1, START)
                    s.activation(o_copy[:, (k - 1) % 2], ps_o, ACT.Copy).then_inc(o_copied, 1)
                if g == 1 and 0 <= new < TILES:
                    wait_round(act, k_formed, c, 2, new + 1)
                    wait_round(act, sum_done, c, 6, 3 * new - 3, START)
                    s.activation(k_split[:, 0, new % 2], k_feat, ACT.Copy).then_inc(k_hi, 1)
                if is_unit(k):
                    wait_round(act, masked, c, 8, k + 1, START)
                    wait_round(act, o_done, c, 8, k - 1, START)
                    s.activation(p_split[:, 0, k % 2], p_mask[:, k % 2], ACT.Copy).then_inc(p_hi, 1)
                if g == 1 and 0 <= new < TILES:
                    wait_round(act, projected, c, 12, proj_index(new, "v") + 1)
                    wait_round(act, o_done, c, 8, KVH * (new - 1), START)
                    s.activation(v_split[:, 0, new % 2], ps_proj[:, proj_index(new, "v") % 2], ACT.Copy
                                 ).then_inc(v_hi, 1)
                if g == 0 and has_state(tile - 1):
                    old = tile - 1
                    wait_round(act, sum_read, c, 6, 3 * old + 3, START)
                    wait_round(act, o_done, c, 8, KVH * (old + 1), START)
                    s.activation(state_split[:, 0, old % 2], state[:, old % 2], ACT.Copy).then_inc(state_hi, 1)
                if is_unit(k + 1):
                    split_transposed(c, tile_of(k + 1), (k + 1) % KVH)
                if transposes_k(k):
                    split_transposed(c, new, "k")
                for t, what in slot_projections(k):
                    if what != "v":
                        exp(c, t, what)

            for k in SLOTS_BEFORE:
                slot(None, k)
            with act.Fori(0, ROUNDS) as c:
                for k in range(1, PER_ROUND + 1):
                    slot(c, k)
            for k in SLOTS_AFTER:
                slot(None, k)

        @block.gpsimd
        def _(pool):
            p = nc.gpsimd
            for counter in (hid_ready, p_ready, o_ready):
                pool.sem_inc(counter, START)
            with pool.Fori(0, B) as b:
                for j in range(FT):
                    pool.wait_ge(hid_hi, b * FT + j + 1)
                    p.tensor_tensor(hid_split[:, 1, j % 2], hid[:, j % 2], hid_split[:, 0, j % 2].bitcast(F32),
                                    ALU.subtract).then_inc(hid_ready, 1)

            pool.wait_ge(w_ready, B * FT)
            pool.wait_ge(hid_ready, B * FT + START)
            for r in range(2):
                p.memset(state_split[:, :, r].bitcast(F32), 0.0).then_inc(state_ready, 1)
            p.memset(k_total, 0.0).then_inc(zeroed, 1)
            p.memset(state, 0.0).then_inc(zeroed, 1)

            def slot(c, k):
                tile, g = tile_of(k), k % KVH
                new = tile + 1
                if is_unit(k - 1):
                    r = (k - 1) % 2
                    wait_round(pool, o_copied, c, 8, k)
                    p.tensor_tensor(o_split[:, 1, r], o_copy[:, r], o_split[:, 0, r].bitcast(F32), ALU.subtract
                                    ).then_inc(o_ready, 1)
                if is_unit(k):
                    wait_round(pool, p_hi, c, 8, k + 1)
                    p.tensor_tensor(p_split[:, 1, k % 2], p_mask[:, k % 2], p_split[:, 0, k % 2].bitcast(F32),
                                    ALU.subtract).then_inc(p_ready, 1)
                for t, what in slot_projections(k):
                    if what != "v":
                        w = rope_index(t, what) % 2
                        wait_round(pool, proj_read, c, 12, proj_index(t, what) + 1)
                        p.tensor_tensor(rope_a[:, w], rope_a[:, w], rope_b[:, w], ALU.add).then_inc(rotated, 1)
                f = k + 2
                if is_unit(f):
                    wait_round(pool, rden_done, c, 8, f + 1)
                    d = rden[:, f % 2].rearrange("p (h o) -> p h o", o=1).broadcast_to([P, REP, P])
                    p.tensor_tensor(heads(q_feat[:, f % 2]), heads(q_feat[:, f % 2]), d, ALU.mult
                                    ).then_inc(normed, 1)

            for k in SLOTS_BEFORE:
                slot(None, k)
            with pool.Fori(0, ROUNDS) as c:
                for k in range(1, PER_ROUND + 1):
                    slot(c, k)
            for k in SLOTS_AFTER:
                slot(None, k)


def constants():
    inv_freq = (1.0 / np.float32(10000.0) ** (np.arange(0, HD, 2, dtype=np.float32) / np.float32(HD)))
    freqs = np.outer(np.arange(S, dtype=np.float32), inv_freq.astype(np.float32)).astype(np.float32)
    cos = np.concatenate([np.cos(freqs)] * 2, -1).reshape(NC, P, HD).transpose(1, 0, 2).reshape(P, -1)
    sin = np.concatenate([-np.sin(freqs), np.sin(freqs)], -1).reshape(NC, P, HD).transpose(1, 0, 2).reshape(P, -1)
    mask = np.triu(np.ones((P, P)))
    return np.concatenate([cos, sin, mask, np.eye(P), np.ones((P, P))], 1).astype(np.float32)


def kernel(L0_attn_x, L0_attn_Wq, L0_attn_Wk, L0_attn_Wv, L0_attn_Wo, L0_ffn_W_up, L0_ffn_W_gate, L0_ffn_W_down):
    import concourse.bacc as bacc
    from concourse.bass_utils import run_bass_kernel_spmd

    def columns(w):
        w = np.asarray(w)
        return w.T.reshape(-1, P, w.shape[0]).transpose(1, 0, 2).reshape(P, -1)

    arrays = {
        "x": np.ascontiguousarray(np.asarray(L0_attn_x)),
        "w_attn": np.ascontiguousarray(np.concatenate(
            [columns(w) for w in (L0_attn_Wk, L0_attn_Wv, L0_attn_Wq, L0_attn_Wo)], 1)),
        "w_ffn": np.ascontiguousarray(np.concatenate(
            [columns(w) for w in (L0_ffn_W_up, L0_ffn_W_gate, L0_ffn_W_down)], 1)),
        "consts": constants(),
    }
    nc = bacc.Bacc("TRN2", target_bir_lowering=False, num_devices=1)
    args = [nc.dram_tensor(n, a.shape, F32, kind="ExternalInput").ap() for n, a in arrays.items()]
    out = nc.dram_tensor("out", (B, S, DM), F32, kind="ExternalOutput").ap()
    build(nc, *args, out)
    r = run_bass_kernel_spmd(nc, [arrays], core_ids=[0])
    return r.results[0]["out"]
```

```python
from contextlib import ExitStack

import concourse.bass as bass
import numpy as np
from concourse import mybir

F32 = mybir.dt.float32
F32R = mybir.dt.float32r
ALU = mybir.AluOpType
ACT = mybir.ActivationFunctionType

P = 128
B, S, DM = 2, 512, 256
H, KVH, HD = 16, 4, 128
REP = H // KVH
FF = 1024
CT = DM // P
NC = S // P
TILES = B * NC
UNITS = TILES * KVH
FT = FF // P
KV = KVH * HD
LN_EPS = 1e-5
LN_STEPS = 8
DEN_EPS = 1e-6
TERN_EPS = 1e-8

W_K = 0
W_V = W_K + CT * KV
W_Q = W_V + CT * KV
W_O = W_Q + CT * H * HD
W_ALL = W_O + H * DM
W_CHUNK = CT * KV
W_CHUNKS = W_ALL // W_CHUNK
T_UP, T_GATE, T_DOWN = 0, CT * FF, 2 * CT * FF
T_ALL = 3 * CT * FF

FFN_STEPS = B * FT
TERN_STEP = {0: [(0, 1)], 1: [(1, 1)], 2: [(2, 1)]}
XT_STEP = 3
W_STEP = {3 + i: i for i in range(W_CHUNKS)}
FILL_STEP = {6: -5, 8: -4, 10: -3, 12: -2, 14: -1}
DOWN_LAG = 2

ROUNDS, PER_ROUND = 3, 2 * KVH
SLOTS_BEFORE = range(0, 3)
LOOP_SLOTS = range(3, 3 + PER_ROUND)
SLOTS_AFTER = range(3 + ROUNDS * PER_ROUND, UNITS + 3)
SCALE_BLOCK = 1.0 / (FF * DM)


START = 1


def wait_round(engine, sem, c, per_round, count, start=0):
    if c is None:
        if count > 0:
            engine.wait_ge(sem, count + start)
    else:
        assert count + start > 0
        engine.wait_ge(sem, c * per_round + count + start)


def tile_of(slot):
    return slot // KVH


def proj_index(tile, what):
    return 6 * tile + {"k": 0, "v": 1}.get(what, 2 + what if isinstance(what, int) else 0)


def rope_index(tile, what):
    return 5 * tile + (0 if what == "k" else 1 + what)


def slot_projections(k):
    new, g = tile_of(k) + 1, k % KVH
    order = {0: [(new, "v"), (new, 0)], 1: [(new, 1)], 2: [(new, 2)], 3: [(new, 3), (new + 1, "k")]}[g]
    return [(t, w) for t, w in order if 0 <= t < TILES]


def slot_rotations(k):
    return [(t, w) for t, w in slot_projections(k) if w != "v"]


def transposes_k(k):
    return k % KVH == 2 and 0 <= tile_of(k) + 1 < TILES


def is_unit(k):
    return 0 <= k < UNITS


def has_state(tile):
    return 0 <= tile < TILES - B


def splits_state(tile):
    return -B <= tile < TILES - B


def build(nc, x, w_attn, w_ffn, consts, out):
    with ExitStack() as ctx:
        def sem(name):
            return ctx.enter_context(nc.semaphore(name))

        r_words = 2 * W_ALL + 2 * CT * B * S + 28 * KV + 2 * 2 * CT * P + 2 * P
        f_tmp = T_ALL + 2 * W_CHUNK + 2 * 512
        f_words = TILES * DM + max(f_tmp, 18 * KV) + 2 * NC * HD + 3 * P
        region_r = ctx.enter_context(nc.sbuf_tensor("region_r", [P, r_words], F32R))
        region_f = ctx.enter_context(nc.sbuf_tensor("region_f", [P, f_words], F32))
        small = ctx.enter_context(nc.sbuf_tensor("small", [P, 160], F32))
        used = {"r": 0, "f": 0}

        def take(region, words):
            at = used[region]
            used[region] += words
            return (region_r if region == "r" else region_f)[:, at:at + words]

        w_split = take("r", 2 * W_ALL).rearrange("p (s n) -> p s n", s=2)
        xt_split = take("r", 2 * CT * B * S).rearrange("p (s c t) -> p s c t", s=2, c=CT)
        shared_r = take("r", 20 * KV)
        tern = shared_r[:, 0:T_ALL]
        o_split = shared_r[:, 0:4 * KV].rearrange("p (s r n) -> p s r n", s=2, r=2)
        by_tile = shared_r[:, 4 * KV:].rearrange("p (r w s n) -> p w s r n", r=2, w=4, s=2)[:, :, :, ::-1]
        v_split, kt_split, k_split, state_split = (by_tile[:, i] for i in range(4))
        assert T_ALL == 12 * KV
        qt_split = take("r", 4 * KV).rearrange("p (s r n) -> p s r n", s=2, r=2)
        p_split = take("r", 4 * KV).rearrange("p (s r n) -> p s r n", s=2, r=2)
        hid_split = p_split
        x_stat = take("r", 2 * 2 * CT * P).rearrange("p (r s c t) -> p r s c t", r=2, s=2, c=CT)
        tri = take("r", P)
        ones = take("r", P)

        acc = take("f", TILES * DM).rearrange("p (t n) -> p t n", t=TILES)
        shared_f = take("f", max(f_tmp, 18 * KV))
        t_raw = shared_f[:, 0:T_ALL]
        w_raw = shared_f[:, T_ALL:T_ALL + 2 * W_CHUNK].rearrange("p (r n) -> p r n", r=2)
        hid = shared_f[:, T_ALL + 2 * W_CHUNK:f_tmp].rearrange("p (r n) -> p r n", r=2)
        xn = shared_f[:, T_ALL:T_ALL + TILES * DM].rearrange("p (t n) -> p t n", t=TILES)
        att = shared_f[:, 0:18 * KV].rearrange("p (b n) -> p b n", n=KV)
        rope_q, rope_k, rope_b = att[:, 0:2], att[:, 2], att[:, 3:5]
        q_feat, k_feat, k_total = att[:, 5:7], att[:, 7], att[:, 8:10]
        z_sum, state = [att[:, 10], att[:, 12]], [att[:, 11], att[:, 13]]
        p_mask, o_copy = att[:, 14:16], att[:, 16:18]
        const_f = take("f", 2 * NC * HD + 3 * P)
        cos_t = const_f[:, 0:NC * HD].rearrange("p (c n) -> p c n", c=NC)
        sin_t = const_f[:, NC * HD:2 * NC * HD].rearrange("p (c n) -> p c n", c=NC)
        mask = const_f[:, 2 * NC * HD:2 * NC * HD + P]
        ident = const_f[:, 2 * NC * HD + P:2 * NC * HD + 2 * P]
        ones_f = const_f[:, 2 * NC * HD + 2 * P:2 * NC * HD + 3 * P]

        stats = small[:, 0:6 * TILES].rearrange("p (t n) -> p t n", t=TILES)
        moments = small[:, 48:48 + 2 * TILES].rearrange("p (t n) -> p t n", t=TILES)
        var, root, rstd, newton = (small[:, 64 + 8 * i:72 + 8 * i] for i in range(4))
        abs_sum = small[:, 96:102]
        scale, thresh, neg_thresh = small[:, 102:105], small[:, 105:108], small[:, 108:111]
        up_scale, gd_scale = small[:, 111:112], small[:, 112:113]
        den = small[:, 120:128].rearrange("p (r h) -> p r h", r=2)
        rden = small[:, 128:136].rearrange("p (r h) -> p r h", r=2)

        bank = ctx.enter_context(nc.psum_tensor("bank", [P, 8, 512], F32))
        ps_total = [bank[:, i, 0:1] for i in (2, 3, 0)]
        ps_xt = [bank[:, i, :] for i in (0, 1, 5, 6)]
        ps_up, ps_gate = bank[:, 2, :], bank[:, 3, :]
        ps_ffn = bank[:, 4:8:3, :].rearrange("p a (h n) -> p a h n", h=2)
        ps_proj, ps_score = bank[:, 0:2, :], bank[:, 2:4, :]
        ps_o, ps_tr, ps_sum, ps_y = bank[:, 4, :], bank[:, 5, :], bank[:, 6, :], bank[:, 7, :]

        x_loaded = [sem(f"x_loaded{b}") for b in range(B)]
        ident_loaded, consts_loaded = sem("ident_loaded"), sem("consts_loaded")
        t_loaded = [sem(f"t_loaded{w}") for w in range(3)]
        w_loaded = [sem(f"w_loaded{r}") for r in range(2)]
        ln_step, root_done = sem("ln_step"), sem("root_done")
        xn_done = [sem(f"xn_done{b}") for b in range(B)]
        abs_done, total_done, tern_step = sem("abs_done"), sem("total_done"), sem("tern_step")
        above = [sem(f"above{w}") for w in range(3)]
        tern_done = [sem(f"tern_done{w}") for w in range(3)]
        xt_done, xt_hi, xt_ready = sem("xt_done"), sem("xt_hi"), sem("xt_ready")
        flags_done = sem("flags_done")
        up_done = sem("up_done")
        gate_done, silu_done, hid_done = sem("gate_done"), sem("silu_done"), sem("hid_done")
        hid_hi, hid_ready, down_done = sem("hid_hi"), sem("hid_ready"), sem("down_done")
        ffn_added, w_hi, w_ready = sem("ffn_added"), sem("w_hi"), sem("w_ready")

        inc_done, inc_read = sem("inc_done"), sem("inc_read")
        x_stat_loaded = [sem(f"x_stat_loaded{r}") for r in range(2)]
        zeroed = sem("zeroed")
        projected, proj_read = sem("projected"), sem("proj_read")
        rotated, clipped, exped = sem("rotated"), sem("clipped"), sem("exped")
        q_formed, den_done, rden_done, normed = (sem(n) for n in ("q_formed", "den_done", "rden_done", "normed"))
        k_formed, k_hi, k_ready = sem("k_formed"), sem("k_hi"), sem("k_ready")
        v_hi = sem("v_hi")
        transposed, tr_hi, tr_ready = sem("transposed"), sem("tr_hi"), sem("tr_ready")
        sum_done, sum_read = sem("sum_done"), sem("sum_read")
        scored, masked, p_hi, p_ready = sem("scored"), sem("masked"), sem("p_hi"), sem("p_ready")
        o_done, o_hi, o_copied, o_ready = sem("o_done"), sem("o_hi"), sem("o_copied"), sem("o_ready")
        state_hi, state_ready = sem("state_hi"), sem("state_ready")
        y_done, y_half, out_ready, out_stored = sem("y_done"), sem("y_half"), sem("out_ready"), sem("out_stored")

        block = ctx.enter_context(nc.Block())

        def heads(ap):
            return ap.rearrange("p (h n) -> p h n", h=REP)

        def rope_a(what):
            return rope_k if what == "k" else rope_q[:, what % 2]

        def rope_b_place(what):
            return 0 if what == "k" else what % 2

        @block.sync
        def _(sp):
            x_in = x.rearrange("b (c p) n -> b p c n", p=P)
            out_v = out.rearrange("b (c p) n -> b p c n", p=P)
            n_const = 2 * NC * HD
            for b in range(B):
                sp.dma_start(acc[:, b * NC:(b + 1) * NC], x_in[b]).then_inc(x_loaded[b], 16)
            sp.dma_start(t_raw[:, T_UP:T_GATE], w_ffn[:, T_UP:T_GATE]).then_inc(t_loaded[0], 16)
            sp.dma_start(const_f[:, n_const:], consts[:, n_const:]).then_inc(ident_loaded, 16)
            sp.dma_start(t_raw[:, T_GATE:T_DOWN], w_ffn[:, T_GATE:T_DOWN]).then_inc(t_loaded[1], 16)
            sp.dma_start(t_raw[:, T_DOWN:], w_ffn[:, T_DOWN:]).then_inc(t_loaded[2], 16)
            sp.dma_start(const_f[:, 0:n_const], consts[:, 0:n_const]).then_inc(consts_loaded, 16)

            sp.wait_ge(xt_done, B * CT)
            for i in range(2):
                sp.dma_start(w_raw[:, i], w_attn[:, i * W_CHUNK:(i + 1) * W_CHUNK]).then_inc(w_loaded[i], 16)

            def load_x_stat(c, tile):
                r = tile % 2
                wait_round(sp, projected, c, 6 * 2, proj_index(tile - 2, 3) + 1)
                chunk = tile // B if c is None else c + tile // B
                sp.dma_start(x_stat[:, r].bitcast(F32),
                             xt_split[:, :, :, bass.ds(chunk * P + (tile % B) * S, P)].bitcast(F32)
                             ).then_inc(x_stat_loaded[r], 16)

            def store(c, tile):
                wait_round(sp, out_ready, c, 2, tile + 1, START)
                chunk = tile // B if c is None else c + tile // B
                b = tile % B
                sp.dma_start(out_v[b][:, bass.ds(chunk, 1), :],
                             acc[:, bass.ds(chunk + b * NC, 1), :]).then_inc(out_stored, 16)

            sp.wait_ge(xt_ready, B * CT)
            load_x_stat(None, 0)
            load_x_stat(None, 1)
            with sp.Fori(0, W_CHUNKS // 2 - 1) as pair:
                for r in range(2):
                    sp.wait_ge(w_ready, pair * 2 + r + 1)
                    sp.dma_start(w_raw[:, r], w_attn[:, bass.ds((pair * 2 + r + 2) * W_CHUNK, W_CHUNK)]
                                 ).then_inc(w_loaded[r], 16)
            with sp.Fori(0, ROUNDS) as c:
                for tile in range(2):
                    load_x_stat(c, tile + 2)
                    store(c, tile)
            for tile in range(TILES - 2, TILES):
                store(None, tile)
            sp.wait_ge(out_stored, 16 * TILES)

        @block.tensor
        def _(pe):
            for counter in (sum_done, inc_done, o_done, y_done):
                pe.sem_inc(counter, START)

            def total(w):
                pe.wait_ge(abs_done, 2 * w + 2)
                for i in range(2):
                    mm = nc.tensor.matmul(ps_total[w], ones_f, abs_sum[:, 2 * w + i:2 * w + i + 1],
                                          start=(i == 0), stop=(i == 1))
                mm.then_inc(total_done, 1)

            def transpose_xn(b):
                pe.wait_ge(xn_done[b], NC)
                for half in range(CT):
                    for t in range(NC):
                        mm = nc.tensor.transpose(ps_xt[CT * b + half][:, t * P:(t + 1) * P],
                                                 xn[:, NC * b + t, half * P:(half + 1) * P], ident)
                    mm.then_inc(xt_done, 1)

            def hidden(step, ps, at):
                b, j = divmod(step, FT)
                for half in range(CT):
                    col = at + half * FF + j * P
                    for lo in range(2):
                        mm = nc.tensor.matmul(ps, tern[:, col:col + P], xt_split[:, lo, half, b * S:(b + 1) * S],
                                              start=(half == 0 and lo == 0), stop=(half == CT - 1 and lo == 1))
                return mm

            def up(step):
                if step < FT:
                    pe.wait_ge(tern_done[0], step // (FT // 2) + 1)
                pe.wait_ge(xt_ready, CT * (step // FT + 1))
                if step:
                    pe.wait_ge(silu_done, step)
                hidden(step, ps_up, T_UP).then_inc(up_done, 1)

            def gate(step):
                if step < FT:
                    pe.wait_ge(tern_done[1], step // (FT // 2) + 1)
                if step:
                    pe.wait_ge(hid_done, step)
                hidden(step, ps_gate, T_GATE).then_inc(gate_done, 1)

            def down(step):
                b, j = divmod(step, FT)
                if b == 0 and j % (FT // 2) == 0:
                    pe.wait_ge(tern_done[2], j // (FT // 2) + 1)
                if j == 0 and b:
                    pe.wait_ge(ffn_added, b)
                pe.wait_ge(hid_ready, b * FT + j + 1)
                for lo in range(2):
                    for t in range(NC):
                        mm = nc.tensor.matmul(ps_ffn[:, t // 2, t % 2], hid_split[:, lo, j % 2, t * P:(t + 1) * P],
                                              tern[:, T_DOWN + j * DM:T_DOWN + (j + 1) * DM],
                                              start=(j == 0 and lo == 0 and t % 2 == 0),
                                              stop=(j == FT - 1 and lo == 1), skip_group_check=True)
                mm.then_inc(down_done, 1)

            def project(c, tile, what):
                r = tile % 2
                n = proj_index(tile, what)
                if what == "k":
                    wait_round(pe, x_stat_loaded[r], c, 16, 16 * (tile // 2 + 1))
                wait_round(pe, proj_read, c, 12, n - 1)
                if what in ("k", "v"):
                    col = W_K if what == "k" else W_V
                    chunk = 0 if what == "k" else 1
                else:
                    col, chunk = W_Q + what * CT * KV, 2 + what
                if c is None and tile == 0:
                    pe.wait_ge(w_ready, chunk + 1)
                passes = [(s, w, half) for half in range(CT) for s, w in ((0, 0), (0, 1), (1, 0))]
                for i, (s, w, half) in enumerate(passes):
                    at = col + half * KV
                    mm = nc.tensor.matmul(ps_proj[:, n % 2], x_stat[:, r, s, half],
                                          w_split[:, w, at:at + KV], start=(i == 0), stop=(i == len(passes) - 1))
                mm.then_inc(projected, 1)

            def transpose(c, tile, what):
                if what == "k":
                    wait_round(pe, k_formed, c, 2, tile + 1)
                    src = k_feat
                else:
                    wait_round(pe, normed, c, 8, KVH * tile + what + 1)
                    src = q_feat[:, what % 2]
                n = rope_index(tile, what)
                wait_round(pe, tr_ready, c, 10, n)
                for h in range(REP):
                    mm = nc.tensor.transpose(ps_tr[:, h * P:(h + 1) * P], src[:, h * P:(h + 1) * P], ident)
                mm.then_inc(transposed, 1)

            def slot(c, k):
                tile, g = tile_of(k), k % KVH
                r, kr = tile % 2, k % 2
                if is_unit(k):
                    wait_round(pe, tr_ready, c, 10, rope_index(tile, g) + 1)
                    wait_round(pe, masked, c, 8, k - 1, START)
                    for i, (s, m) in enumerate(((0, 0), (0, 1), (1, 0))):
                        mm = nc.tensor.matmul(ps_score[:, kr], kt_split[:, s, r, g * P:(g + 1) * P],
                                              qt_split[:, m, kr], start=(i == 0), stop=(i == 2))
                    mm.then_inc(scored, 1)
                projections = slot_projections(k)
                for t, what in projections[:1]:
                    project(c, t, what)
                if is_unit(k + 1):
                    transpose(c, tile_of(k + 1), (k + 1) % KVH)
                for t, what in projections[1:]:
                    project(c, t, what)
                e = k - 2
                if is_unit(e):
                    wait_round(pe, o_hi, c, 8, e + 1)
                    tw, gw, pr = tile_of(e), e % KVH, e % 2
                    if gw == 0:
                        wait_round(pe, out_ready, c, 2, tw, START)
                    for s in range(2):
                        if s == 1:
                            wait_round(pe, o_ready, c, 8, e + 1, START)
                        for h in range(REP):
                            at = W_O + (gw * REP + h) * DM
                            first, last = gw == 0 and s == 0 and h == 0, gw == KVH - 1 and s == 1 and h == REP - 1
                            o_st = o_split[:, s, pr, h * P:(h + 1) * P]
                            if s == 0:
                                mm = nc.tensor.matmul(ps_y.rearrange("p (w n) -> p w n", w=2), o_st,
                                                      w_split[:, :, at:at + DM], start=first, stop=last)
                            else:
                                mm = nc.tensor.matmul(ps_y[:, 0:DM], o_st, w_split[:, 0, at:at + DM],
                                                      start=first, stop=last)
                    mm.then_inc(y_done, 1)
                if (g == 1 and 0 <= tile + 1 < TILES) or (g == 2 and has_state(tile + 1)):
                    new = tile + 1
                    wait_round(pe, k_ready, c, 2, new + 1)
                    wait_round(pe, sum_read, c, 4, 2 * new + g - 1, START)
                    if g == 1:
                        wait_round(pe, inc_read, c, 2, new - 1, START)
                    for s in range(2):
                        mm = nc.tensor.matmul(ps_sum, tri if g == 1 else ones, k_split[:, s, new % 2],
                                              start=(s == 0), stop=(s == 1))
                    mm.then_inc(sum_done, 1)
                if g == 3 and has_state(tile):
                    wait_round(pe, sum_read, c, 4, 2 * tile + 4, START)
                    wait_round(pe, proj_read, c, 12, proj_index(tile, "v") + 1)
                    for j in range(KVH):
                        cols = slice(j * P, (j + 1) * P)
                        for i, (s, m) in enumerate(((0, 0), (0, 1), (1, 0))):
                            mm = nc.tensor.matmul(ps_sum[:, cols], k_split[:, s, r, cols], v_split[:, m, r, cols],
                                                  start=(i == 0), stop=(i == 2))
                    mm.then_inc(inc_done, 1)
                if transposes_k(k):
                    transpose(c, tile + 1, "k")
                if is_unit(k):
                    wait_round(pe, o_copied, c, 8, k)
                    wait_round(pe, state_ready, c, 2, tile + 1)
                    for i, (s, m) in enumerate(((0, 0), (0, 1), (1, 0))):
                        nc.tensor.matmul(ps_o, state_split[:, s, r, g * P:(g + 1) * P], qt_split[:, m, kr],
                                         start=(i == 0), stop=False)
                    wait_round(pe, proj_read, c, 12, proj_index(tile, "v") + 1)
                    wait_round(pe, p_hi, c, 8, k + 1)
                    for s in range(2):
                        nc.tensor.matmul(ps_o, v_split[:, s, r, g * P:(g + 1) * P], p_split[:, 0, kr],
                                         start=False, stop=False)
                    wait_round(pe, p_ready, c, 8, k + 1, START)
                    nc.tensor.matmul(ps_o, v_split[:, 0, r, g * P:(g + 1) * P], p_split[:, 1, kr],
                                     start=False, stop=True).then_inc(o_done, 1)

            pe.wait_ge(ident_loaded, 16)
            total(0)
            transpose_xn(0)
            for step in range(FFN_STEPS):
                up(step)
                if step == 0:
                    total(1)
                    total(2)
                    transpose_xn(1)
                gate(step)
                if step >= DOWN_LAG:
                    down(step - DOWN_LAG)
                if step in FILL_STEP:
                    if step == min(FILL_STEP):
                        pe.wait_ge(tern_step, 1 + 3 * 2)
                        pe.wait_ge(flags_done, 2)
                    slot(None, FILL_STEP[step])
            for step in range(FFN_STEPS - DOWN_LAG, FFN_STEPS):
                down(step)
            pe.wait_ge(w_ready, W_CHUNKS)
            pe.wait_ge(ffn_added, B)
            for k in SLOTS_BEFORE:
                slot(None, k)
            with pe.Fori(0, ROUNDS) as c:
                for k in LOOP_SLOTS:
                    slot(c, k)
            for k in SLOTS_AFTER:
                slot(None, k)

        @block.vector
        def _(dve):
            v = nc.vector
            for counter in (masked, sum_read, inc_read, out_ready):
                dve.sem_inc(counter, START)
            step = [0]

            def chained(sem, ins):
                step[0] += 1
                ins.then_inc(sem, 1)
                dve.wait_ge(sem, step[0])

            for t in range(TILES):
                if t % NC == 0:
                    dve.wait_ge(x_loaded[t // NC], 16)
                ins = v.bn_stats(stats[:, t], acc[:, t])
            chained(ln_step, ins)
            for t in range(TILES):
                ins = v.bn_aggr(moments[:, t], stats[:, t])
            chained(ln_step, ins)
            chained(ln_step, v.tensor_scalar(var, moments[:, :, 1], LN_EPS, None, ALU.add))
            dve.wait_ge(root_done, 1)
            chained(ln_step, v.reciprocal(rstd, root))
            chained(ln_step, v.tensor_tensor(newton, rstd, rstd, ALU.mult))
            chained(ln_step, v.tensor_tensor(newton, newton, var, ALU.mult))
            chained(ln_step, v.tensor_scalar(newton, newton, -0.5, 1.5, ALU.mult, ALU.add))
            chained(ln_step, v.tensor_tensor(rstd, rstd, newton, ALU.mult))
            for t in range(NC):
                v.tensor_scalar(xn[:, t], acc[:, t], moments[:, t, 0:1], rstd[:, t:t + 1],
                                ALU.subtract, ALU.mult).then_inc(xn_done[0], 1)

            step[0] = 0

            def threshold(w):
                one = slice(w, w + 1)
                dve.wait_ge(total_done, w + 1)
                chained(tern_step, v.tensor_scalar(scale[:, one], ps_total[w], SCALE_BLOCK, TERN_EPS,
                                                   ALU.mult, ALU.add))
                v.tensor_scalar(thresh[:, one], scale[:, one], 0.5, None, ALU.mult)
                chained(tern_step, v.tensor_scalar(neg_thresh[:, one], scale[:, one], -0.5, None, ALU.mult))
                if w == 0:
                    chained(tern_step, v.tensor_scalar(up_scale, scale[:, one], -1.0, None, ALU.mult))

            def ternary(w, half):
                def view(region):
                    if w == 2:
                        at = T_DOWN + half * FF
                        return region[:, at:at + FF]
                    at = (T_UP, T_GATE)[w]
                    return region[:, at:at + CT * FF].rearrange("p (c h n) -> p c h n", c=CT, h=2)[:, :, half]

                one = slice(w, w + 1)
                v.tensor_scalar(view(tern), view(t_raw), thresh[:, one], None, ALU.is_gt).then_inc(above[w], 1)
                dve.wait_ge(above[w], half + 1)
                v.scalar_tensor_tensor(view(tern), view(t_raw), neg_thresh[:, one], view(tern).bitcast(F32),
                                       ALU.is_lt, ALU.subtract).then_inc(tern_done[w], 1)

            def split_xt(b):
                for half in range(CT):
                    dve.wait_ge(xt_hi, b * CT + half + 1)
                    dst = xt_split[:, :, half, b * S:(b + 1) * S]
                    v.tensor_tensor(dst[:, 1], ps_xt[b * CT + half], dst[:, 0].bitcast(F32), ALU.subtract
                                    ).then_inc(xt_ready, 1)

            threshold(0)
            ternary(0, 0)
            split_xt(0)
            threshold(1)
            ternary(1, 0)
            threshold(2)
            chained(tern_step, v.tensor_tensor(gd_scale, scale[:, 1:2], scale[:, 2:3], ALU.mult))
            ternary(2, 0)

            def ffn_step(step):
                b, j = divmod(step, FT)
                dve.wait_ge(gate_done, step + 1)
                dve.wait_ge(silu_done, step + 1)
                v.scalar_tensor_tensor(hid[:, j % 2], ps_gate, gd_scale, hid[:, j % 2],
                                       ALU.mult, ALU.mult).then_inc(hid_done, 1)
                for w, half in TERN_STEP.get(step, ()):
                    ternary(w, half)
                if step == XT_STEP:
                    split_xt(1)
                if step in W_STEP:
                    i = W_STEP[step]
                    cols = slice(i * W_CHUNK, (i + 1) * W_CHUNK)
                    dve.wait_ge(w_hi, i + 1)
                    v.tensor_tensor(w_split[:, 1, cols], w_raw[:, i % 2], w_split[:, 0, cols].bitcast(F32),
                                    ALU.subtract).then_inc(w_ready, 1)

            def add_ffn(b):
                dve.wait_ge(down_done, (b + 1) * FT)
                for i in range(2):
                    half = acc[:, b * NC + 2 * i:b * NC + 2 * i + 2]
                    ins = v.tensor_tensor(half, ps_ffn[:, i], half, ALU.add)
                ins.then_inc(ffn_added, 1)

            def rotate(c, tile, what):
                n = proj_index(tile, what)
                chunk = tile // B if c is None else c + tile // B
                wait_round(dve, projected, c, 12, n + 1)
                src = ps_proj[:, n % 2]
                v.tensor_tensor(heads(rope_a(what)), heads(src),
                                cos_t[:, bass.ds(chunk, 1), :].broadcast_to([P, REP, HD]), ALU.mult)
                swapped = src.rearrange("p (h u e) -> p h u e", h=REP, u=2)[:, :, ::-1, :]
                sin = sin_t[:, bass.ds(chunk, 1), :].rearrange("p o (u e) -> p o u e", u=2)
                if what == 0:
                    wait_round(dve, rotated, c, 10, rope_index(tile, "k") + 1)
                v.tensor_tensor(rope_b[:, rope_b_place(what)].rearrange("p (h u e) -> p h u e", h=REP, u=2), swapped,
                                sin.broadcast_to([P, REP, 2, HD // 2]), ALU.mult).then_inc(proj_read, 1)

            def split_transposed(c, tile, what):
                w = rope_index(tile, what)
                wait_round(dve, tr_hi, c, 10, w + 1)
                dst = kt_split[:, :, tile % 2] if what == "k" else qt_split[:, :, what % 2]
                v.tensor_tensor(dst[:, 1], ps_tr, dst[:, 0].bitcast(F32), ALU.subtract).then_inc(tr_ready, 1)

            def slot(c, k):
                tile, g = tile_of(k), k % KVH
                new = tile + 1
                if g == 1 and 0 <= new < TILES:
                    wait_round(dve, exped, c, 10, rope_index(new, "k") + 1)
                    v.scalar_tensor_tensor(k_feat, rope_k, 1.0, k_feat,
                                           ALU.add, ALU.max).then_inc(k_formed, 1)
                f = k + 2
                if is_unit(f):
                    ft, fg, fr = tile_of(f), f % KVH, f % 2
                    wait_round(dve, exped, c, 10, rope_index(ft, fg) + 1)
                    v.scalar_tensor_tensor(q_feat[:, fr], rope_q[:, fr], 1.0, q_feat[:, fr],
                                           ALU.add, ALU.max).then_inc(q_formed, 1)
                if is_unit(k):
                    wait_round(dve, scored, c, 8, k + 1)
                    wait_round(dve, p_ready, c, 8, k - 1, START)
                    v.tensor_tensor(heads(p_mask[:, k % 2]), heads(ps_score[:, k % 2]),
                                    mask.rearrange("p (o n) -> p o n", o=1).broadcast_to([P, REP, P]),
                                    ALU.mult).then_inc(masked, 1)
                if g == 1 and 0 <= new < TILES:
                    wait_round(dve, k_hi, c, 2, new + 1)
                    v.tensor_tensor(k_split[:, 1, new % 2], k_feat, k_split[:, 0, new % 2].bitcast(F32),
                                    ALU.subtract).then_inc(k_ready, 1)
                if is_unit(f):
                    wait_round(dve, q_formed, c, 8, f + 1)
                    wait_round(dve, sum_read, c, 4, 2 * ft + 1, START)
                    wait_round(dve, normed, c, 8, f - 1)
                    wait_round(dve, rotated, c, 10, rope_index(*divmod(min(f + 1, UNITS - 1), KVH)) + 1)
                    for h in range(REP):
                        cols = slice(h * P, (h + 1) * P)
                        ins = v.tensor_tensor_reduce(out=rope_b[:, (fr + 1) % 2, cols], in0=q_feat[:, fr, cols],
                                                     in1=z_sum[ft % 2][:, fg * P:(fg + 1) * P], scale=1.0,
                                                     scalar=DEN_EPS, op0=ALU.mult, op1=ALU.add,
                                                     accum_out=den[:, fr, h:h + 1])
                    ins.then_inc(den_done, 1)
                if g == 2 and 0 <= tile - 1 < TILES:
                    old = tile - 1
                    wait_round(dve, y_done, c, 8, KVH * old + KVH, START)
                    chunk = old // B if c is None else c + old // B
                    dst = acc[:, bass.ds(chunk + (old % B) * NC, 1), :]
                    y = ps_y.rearrange("p (w n) -> p w n", w=2)
                    v.tensor_tensor(dst, y[:, 0:1], dst, ALU.add).then_inc(y_half, 1)
                    wait_round(dve, y_half, c, 2, old + 1)
                    v.tensor_tensor(dst, y[:, 1:2], dst, ALU.add).then_inc(out_ready, 1)
                projections = slot_projections(k)
                if not projections and is_unit(k + 1):
                    split_transposed(c, tile_of(k + 1), (k + 1) % KVH)
                for i, (t, what) in enumerate(projections):
                    if i == 1 and is_unit(k + 1):
                        split_transposed(c, tile_of(k + 1), (k + 1) % KVH)
                    if what == "v":
                        wait_round(dve, v_hi, c, 2, t + 1)
                        v.tensor_tensor(v_split[:, 1, t % 2], ps_proj[:, proj_index(t, what) % 2],
                                        v_split[:, 0, t % 2].bitcast(F32), ALU.subtract).then_inc(proj_read, 1)
                    else:
                        rotate(c, t, what)
                    if i == 0 and is_unit(f):
                        wait_round(dve, den_done, c, 8, f + 1)
                        v.reciprocal(rden[:, fr], den[:, fr]).then_inc(rden_done, 1)
                if not projections and is_unit(f):
                    wait_round(dve, den_done, c, 8, f + 1)
                    v.reciprocal(rden[:, fr], den[:, fr]).then_inc(rden_done, 1)
                if len(projections) == 1 and is_unit(k + 1):
                    split_transposed(c, tile_of(k + 1), (k + 1) % KVH)
                if g == 1 and 0 <= new < TILES:
                    wait_round(dve, sum_done, c, 4, 2 * new + 1, START)
                    wait_round(dve, sum_read, c, 4, 2 * new - 2, START)
                    v.tensor_tensor(z_sum[new % 2], ps_sum, k_total[:, new % 2], ALU.add).then_inc(sum_read, 1)
                if g == 2 and has_state(new):
                    wait_round(dve, sum_done, c, 4, 2 * new + 2, START)
                    v.tensor_tensor(k_total[:, new % 2], ps_sum, k_total[:, new % 2], ALU.add
                                    ).then_inc(sum_read, 1)
                if transposes_k(k):
                    split_transposed(c, new, "k")
                if g == 0 and splits_state(tile - 1):
                    old = tile - 1
                    wait_round(dve, state_hi, c, 2, old + B + 1)
                    v.tensor_tensor(state_split[:, 1, old % 2], state[old % 2],
                                    state_split[:, 0, old % 2].bitcast(F32), ALU.subtract).then_inc(state_ready, 1)
                if g == 3 and has_state(tile):
                    wait_round(dve, inc_done, c, 2, tile + 1, START)
                    wait_round(dve, state_ready, c, 2, tile + 1)
                    v.tensor_tensor(state[tile % 2], ps_sum, state[tile % 2], ALU.add).then_inc(inc_read, 1)
            for step in range(FFN_STEPS):
                ffn_step(step)
                if step % FT == DOWN_LAG - 1 and step > FT:
                    add_ffn(step // FT - 1)
                if step in FILL_STEP:
                    if step == min(FILL_STEP):
                        dve.wait_ge(consts_loaded, 16)
                        dve.wait_ge(zeroed, 2)
                    slot(None, FILL_STEP[step])
            add_ffn(B - 1)
            dve.wait_ge(zeroed, 3)
            for k in SLOTS_BEFORE:
                slot(None, k)
            with dve.Fori(0, ROUNDS) as c:
                for k in LOOP_SLOTS:
                    slot(c, k)
            for k in SLOTS_AFTER:
                slot(None, k)

        @block.scalar
        def _(act):
            s = nc.scalar
            act.wait_ge(ln_step, 3)
            s.activation(root, var, ACT.Sqrt).then_inc(root_done, 1)

            def abs_sums(w):
                act.wait_ge(t_loaded[w], 16)
                for i in range(2 * w, 2 * w + 2):
                    if i:
                        act.wait_ge(abs_done, i)
                    s.activation(hid, t_raw[:, i * FF:(i + 1) * FF].rearrange("p (r n) -> p r n", r=2), ACT.Abs,
                                 accum_out=abs_sum[:, i:i + 1]).then_inc(abs_done, 1)

            def xt_hi_of(b):
                for half in range(CT):
                    act.wait_ge(xt_done, b * CT + half + 1)
                    s.activation(xt_split[:, 0, half, b * S:(b + 1) * S], ps_xt[b * CT + half],
                                 ACT.Copy).then_inc(xt_hi, 1)

            abs_sums(0)
            xt_hi_of(0)
            abs_sums(1)
            abs_sums(2)
            xt_hi_of(1)
            s.activation(tri, mask, ACT.Copy).then_inc(flags_done, 1)
            s.activation(ones, ones_f, ACT.Copy).then_inc(flags_done, 1)
            act.wait_ge(abs_done, 6)
            act.wait_ge(tern_step, 3)

            def ffn_step(step):
                b, j = divmod(step, FT)
                act.wait_ge(up_done, step + 1)
                if step >= 2:
                    act.wait_ge(hid_ready, step - 1)
                s.activation(hid[:, j % 2], ps_up, ACT.Silu, scale=up_scale).then_inc(silu_done, 1)
                act.wait_ge(hid_done, step + 1)
                if step >= 2:
                    act.wait_ge(down_done, step - 1)
                s.activation(hid_split[:, 0, j % 2], hid[:, j % 2], ACT.Copy).then_inc(hid_hi, 1)
                if step + 1 in W_STEP:
                    i = W_STEP[step + 1]
                    act.wait_ge(w_loaded[i % 2], (i // 2 + 1) * 16)
                    s.activation(w_split[:, 0, i * W_CHUNK:(i + 1) * W_CHUNK], w_raw[:, i % 2], ACT.Copy
                                 ).then_inc(w_hi, 1)

            def exp(c, tile, what):
                w = rope_index(tile, what)
                wait_round(act, rotated, c, 10, w + 1)
                if what == "k":
                    wait_round(act, transposed, c, 10, rope_index(tile - 1, "k") + 1)
                    wait_round(act, k_ready, c, 2, tile)
                    dst = k_feat
                else:
                    wait_round(act, transposed, c, 10, rope_index(*divmod(KVH * tile + what - 2, KVH)) + 1)
                    dst = q_feat[:, what % 2]
                s.activation(dst, rope_a(what), ACT.Relu, scale=-1.0).then_inc(clipped, 1)
                wait_round(act, clipped, c, 10, w + 1)
                s.activation(dst, dst, ACT.Exp, scale=-1.0).then_inc(exped, 1)

            def split_transposed(c, tile, what):
                wait_round(act, transposed, c, 10, rope_index(tile, what) + 1)
                if what == "k":
                    wait_round(act, o_done, c, 8, KVH * (tile - 1), START)
                    dst = kt_split[:, 0, tile % 2]
                else:
                    wait_round(act, o_done, c, 8, KVH * tile + what - 1, START)
                    dst = qt_split[:, 0, what % 2]
                s.activation(dst, ps_tr, ACT.Copy).then_inc(tr_hi, 1)

            def slot(c, k):
                tile, g = tile_of(k), k % KVH
                new = tile + 1
                if is_unit(k - 1):
                    wait_round(act, o_done, c, 8, k, START)
                    wait_round(act, y_done, c, 8, k - 2, START)
                    s.activation(o_split[:, 0, (k - 1) % 2], ps_o, ACT.Copy).then_inc(o_hi, 1)
                    wait_round(act, o_ready, c, 8, k - 1, START)
                    s.activation(o_copy[:, (k - 1) % 2], ps_o, ACT.Copy).then_inc(o_copied, 1)
                if g == 1 and 0 <= new < TILES:
                    wait_round(act, k_formed, c, 2, new + 1)
                    wait_round(act, inc_done, c, 2, new - 1, START)
                    s.activation(k_split[:, 0, new % 2], k_feat, ACT.Copy).then_inc(k_hi, 1)
                if is_unit(k):
                    wait_round(act, masked, c, 8, k + 1, START)
                    wait_round(act, o_done, c, 8, k - 1, START)
                    s.activation(p_split[:, 0, k % 2], p_mask[:, k % 2], ACT.Copy).then_inc(p_hi, 1)
                if g == 0 and 0 <= new < TILES:
                    wait_round(act, projected, c, 12, proj_index(new, "v") + 1)
                    wait_round(act, o_done, c, 8, KVH * (new - 1), START)
                    s.activation(v_split[:, 0, new % 2], ps_proj[:, proj_index(new, "v") % 2], ACT.Copy
                                 ).then_inc(v_hi, 1)
                if is_unit(k + 1):
                    split_transposed(c, tile_of(k + 1), (k + 1) % KVH)
                if transposes_k(k):
                    split_transposed(c, new, "k")
                for t, what in slot_rotations(k - 1):
                    exp(c, t, what)
                if g == 0 and splits_state(tile - 1):
                    old = tile - 1
                    if old < 0 and c is None:
                        act.wait_ge(zeroed, old + B + 2)
                    wait_round(act, inc_read, c, 2, old + 1, START)
                    wait_round(act, o_done, c, 8, KVH * (old + 1), START)
                    s.activation(state_split[:, 0, old % 2], state[old % 2], ACT.Copy).then_inc(state_hi, 1)

            for step in range(FFN_STEPS):
                ffn_step(step)
                if step in FILL_STEP:
                    slot(None, FILL_STEP[step])
            for k in SLOTS_BEFORE:
                slot(None, k)
            with act.Fori(0, ROUNDS) as c:
                for k in LOOP_SLOTS:
                    slot(c, k)
            for k in SLOTS_AFTER:
                slot(None, k)

        @block.gpsimd
        def _(pool):
            p = nc.gpsimd
            for counter in (p_ready, o_ready):
                pool.sem_inc(counter, START)

            pool.wait_ge(ln_step, LN_STEPS)
            for t in range(NC, TILES):
                p.tensor_scalar(xn[:, t], acc[:, t], moments[:, t, 0:1], rstd[:, t:t + 1],
                                ALU.subtract, ALU.mult).then_inc(xn_done[1], 1)

            def ffn_step(step):
                j = step % FT
                pool.wait_ge(hid_hi, step + 1)
                p.tensor_tensor(hid_split[:, 1, j % 2], hid[:, j % 2], hid_split[:, 0, j % 2].bitcast(F32),
                                ALU.subtract).then_inc(hid_ready, 1)

            def slot(c, k):
                tile, g = tile_of(k), k % KVH
                new = tile + 1
                if is_unit(k - 1):
                    r = (k - 1) % 2
                    wait_round(pool, o_copied, c, 8, k)
                    p.tensor_tensor(o_split[:, 1, r], o_copy[:, r], o_split[:, 0, r].bitcast(F32), ALU.subtract
                                    ).then_inc(o_ready, 1)
                if is_unit(k):
                    wait_round(pool, p_hi, c, 8, k + 1)
                    p.tensor_tensor(p_split[:, 1, k % 2], p_mask[:, k % 2], p_split[:, 0, k % 2].bitcast(F32),
                                    ALU.subtract).then_inc(p_ready, 1)
                f = k + 2
                if is_unit(f):
                    wait_round(pool, rden_done, c, 8, f + 1)
                    d = rden[:, f % 2].rearrange("p (h o) -> p h o", o=1).broadcast_to([P, REP, P])
                    p.tensor_tensor(heads(q_feat[:, f % 2]), heads(q_feat[:, f % 2]), d, ALU.mult
                                    ).then_inc(normed, 1)
                for t, what in slot_rotations(k):
                    wait_round(pool, proj_read, c, 12, proj_index(t, what) + 1)
                    p.tensor_tensor(rope_a(what), rope_a(what), rope_b[:, rope_b_place(what)], ALU.add
                                    ).then_inc(rotated, 1)

            for step in range(FFN_STEPS):
                ffn_step(step)
                if step in FILL_STEP:
                    if step == min(FILL_STEP):
                        for w in range(3):
                            pool.wait_ge(tern_done[w], 2)
                        p.memset(k_total, 0.0).then_inc(zeroed, 1)
                        p.memset(state[0], 0.0).then_inc(zeroed, 1)
                    slot(None, FILL_STEP[step])
            pool.wait_ge(w_ready, W_CHUNKS)
            p.memset(state[1], 0.0).then_inc(zeroed, 1)
            for k in SLOTS_BEFORE:
                slot(None, k)
            with pool.Fori(0, ROUNDS) as c:
                for k in LOOP_SLOTS:
                    slot(c, k)
            for k in SLOTS_AFTER:
                slot(None, k)


def constants():
    inv_freq = (1.0 / np.float32(10000.0) ** (np.arange(0, HD, 2, dtype=np.float32) / np.float32(HD)))
    freqs = np.outer(np.arange(S, dtype=np.float32), inv_freq.astype(np.float32)).astype(np.float32)
    cos = np.concatenate([np.cos(freqs)] * 2, -1).reshape(NC, P, HD).transpose(1, 0, 2).reshape(P, -1)
    sin = np.concatenate([-np.sin(freqs), np.sin(freqs)], -1).reshape(NC, P, HD).transpose(1, 0, 2).reshape(P, -1)
    mask = np.triu(np.ones((P, P)))
    return np.concatenate([cos, sin, mask, np.eye(P), np.ones((P, P))], 1).astype(np.float32)


def kernel(L0_attn_x, L0_attn_Wq, L0_attn_Wk, L0_attn_Wv, L0_attn_Wo, L0_ffn_W_up, L0_ffn_W_gate, L0_ffn_W_down):
    import concourse.bacc as bacc
    from concourse.bass_utils import run_bass_kernel_spmd

    def columns(w):
        w = np.asarray(w)
        return w.T.reshape(-1, P, w.shape[0]).transpose(1, 0, 2).reshape(P, -1)

    arrays = {
        "x": np.ascontiguousarray(np.asarray(L0_attn_x)),
        "w_attn": np.ascontiguousarray(np.concatenate(
            [columns(w) for w in (L0_attn_Wk, L0_attn_Wv, *np.split(np.asarray(L0_attn_Wq), KVH), L0_attn_Wo)], 1)),
        "w_ffn": np.ascontiguousarray(np.concatenate(
            [columns(w) for w in (L0_ffn_W_up, L0_ffn_W_gate, L0_ffn_W_down)], 1)),
        "consts": constants(),
    }
    nc = bacc.Bacc("TRN2", target_bir_lowering=False, num_devices=1)
    args = [nc.dram_tensor(n, a.shape, F32, kind="ExternalInput").ap() for n, a in arrays.items()]
    out = nc.dram_tensor("out", (B, S, DM), F32, kind="ExternalOutput").ap()
    build(nc, *args, out)
    r = run_bass_kernel_spmd(nc, [arrays], core_ids=[0])
    return r.results[0]["out"]
```

```python
from contextlib import ExitStack

import concourse.bass as bass
import numpy as np
from concourse import mybir

F32 = mybir.dt.float32
F32R = mybir.dt.float32r
ALU = mybir.AluOpType
ACT = mybir.ActivationFunctionType

P = 128
B, S, DM = 2, 512, 256
H, KVH, HD = 16, 4, 128
REP = H // KVH
FF = 1024
CT = DM // P
NC = S // P
TILES = B * NC
UNITS = TILES * KVH
FT = FF // P
KV = KVH * HD
LN_EPS = 1e-5
LN_STEPS = 8
DEN_EPS = 1e-6
TERN_EPS = 1e-8

W_K = 0
W_V = W_K + CT * KV
W_Q = W_V + CT * KV
W_O = W_Q + CT * H * HD
W_ALL = W_O + H * DM
W_CHUNK = CT * KV
W_CHUNKS = W_ALL // W_CHUNK
T_UP, T_GATE, T_DOWN = 0, CT * FF, 2 * CT * FF
T_ALL = 3 * CT * FF

FFN_STEPS = B * FT
TERN_STEP = {0: (2, 0), 1: (0, 1), 2: (1, 1), 3: (2, 1)}
ABOVE_ON_POOL = ((0, 1), (1, 1), (2, 1))
XN_ON_POOL = 2
XT_STEP = 4
W_STEP = {2: 0, 4: 1, 5: 2, 6: 3, 7: 4, 8: 5, 9: 6, 11: 7, 13: 8, 15: 9}
W_ON_POOL = (0, 1, 3, 5, 7)
W_PLACE = (0, 1, 2, 3, 0, 1, 2, 0, 1, 0)
FILL_STEP = {6: -5, 8: -4, 10: -3, 12: -2, 14: -1}
DOWN_LAG = 2

ROUNDS, PER_ROUND = 3, 2 * KVH
SLOTS_BEFORE = range(0, 3)
LOOP_SLOTS = range(3, 3 + PER_ROUND)
SLOTS_AFTER = range(3 + ROUNDS * PER_ROUND, UNITS + 3)
SCALE_BLOCK = 1.0 / (FF * DM)


START = 1


def wait_round(engine, sem, c, per_round, count, start=0):
    if c is None:
        if count > 0:
            engine.wait_ge(sem, count + start)
    else:
        assert count + start > 0
        engine.wait_ge(sem, c * per_round + count + start)


def tile_of(slot):
    return slot // KVH


def proj_index(tile, what):
    return 6 * tile + {"k": 0, "v": 1}.get(what, 2 + what if isinstance(what, int) else 0)


def rope_index(tile, what):
    return 5 * tile + (0 if what == "k" else 1 + what)


def slot_projections(k):
    new, g = tile_of(k) + 1, k % KVH
    order = {0: [(new, "v"), (new, 0)], 1: [(new, 1)], 2: [(new, 2)], 3: [(new, 3), (new + 1, "k")]}[g]
    return [(t, w) for t, w in order if 0 <= t < TILES]


def slot_rotations(k):
    return [(t, w) for t, w in slot_projections(k) if w != "v"]


def transposes_k(k):
    return k % KVH == 2 and 0 <= tile_of(k) + 1 < TILES


def is_unit(k):
    return 0 <= k < UNITS


def has_state(tile):
    return 0 <= tile < TILES - B


def splits_state(tile):
    return -B <= tile < TILES - B


def build(nc, x, w_attn, w_ffn, consts, out):
    with ExitStack() as ctx:
        def sem(name):
            return ctx.enter_context(nc.semaphore(name))

        r_words = 2 * W_ALL + 2 * CT * B * S + 28 * KV + 2 * 2 * CT * P + 2 * P
        f_tmp = T_ALL + TILES * DM + 2 * S
        f_words = TILES * DM + max(f_tmp, 18 * KV) + 2 * NC * HD + 3 * P
        region_r = ctx.enter_context(nc.sbuf_tensor("region_r", [P, r_words], F32R))
        region_f = ctx.enter_context(nc.sbuf_tensor("region_f", [P, f_words], F32))
        small = ctx.enter_context(nc.sbuf_tensor("small", [P, 160], F32))
        used = {"r": 0, "f": 0}

        def take(region, words):
            at = used[region]
            used[region] += words
            return (region_r if region == "r" else region_f)[:, at:at + words]

        w_split = take("r", 2 * W_ALL).rearrange("p (s n) -> p s n", s=2)
        xt_split = take("r", 2 * CT * B * S).rearrange("p (s c t) -> p s c t", s=2, c=CT)
        shared_r = take("r", 20 * KV)
        tern = shared_r[:, 0:T_ALL]
        o_split = shared_r[:, 0:4 * KV].rearrange("p (s r n) -> p s r n", s=2, r=2)
        by_tile = shared_r[:, 4 * KV:].rearrange("p (r w s n) -> p w s r n", r=2, w=4, s=2)[:, :, :, ::-1]
        v_split, kt_split, k_split, state_split = (by_tile[:, i] for i in range(4))
        assert T_ALL == 12 * KV
        qt_split = take("r", 4 * KV).rearrange("p (s r n) -> p s r n", s=2, r=2)
        p_split = take("r", 4 * KV).rearrange("p (s r n) -> p s r n", s=2, r=2)
        hid_split = p_split
        x_stat = take("r", 2 * 2 * CT * P).rearrange("p (r s c t) -> p r s c t", r=2, s=2, c=CT)
        tri = take("r", P)
        ones = take("r", P)

        acc = take("f", TILES * DM).rearrange("p (t n) -> p t n", t=TILES)
        shared_f = take("f", max(f_tmp, 18 * KV))
        t_raw = shared_f[:, 0:T_ALL]
        xn = shared_f[:, T_ALL:T_ALL + TILES * DM].rearrange("p (t n) -> p t n", t=TILES)
        hid = shared_f[:, T_ALL + TILES * DM:f_tmp].rearrange("p (r n) -> p r n", r=2)
        att = shared_f[:, 0:18 * KV].rearrange("p (b n) -> p b n", n=KV)
        rope_q, rope_k, rope_b = att[:, 0:2], att[:, 2], att[:, 3:5]
        q_feat, k_feat, k_total = att[:, 5:7], att[:, 7], att[:, 8:10]
        z_sum, state = [att[:, 10], att[:, 12]], [att[:, 11], att[:, 13]]
        p_mask, o_copy = att[:, 14:16], att[:, 16:18]
        w_raw = [att[:, i:i + 2] for i in (12, 14, 5, 0)]
        assert W_CHUNK == 2 * KV
        const_f = take("f", 2 * NC * HD + 3 * P)
        cos_t = const_f[:, 0:NC * HD].rearrange("p (c n) -> p c n", c=NC)
        sin_t = const_f[:, NC * HD:2 * NC * HD].rearrange("p (c n) -> p c n", c=NC)
        mask = const_f[:, 2 * NC * HD:2 * NC * HD + P]
        ident = const_f[:, 2 * NC * HD + P:2 * NC * HD + 2 * P]
        ones_f = const_f[:, 2 * NC * HD + 2 * P:2 * NC * HD + 3 * P]

        stats = small[:, 0:6 * TILES].rearrange("p (t n) -> p t n", t=TILES)
        moments = small[:, 48:48 + 2 * TILES].rearrange("p (t n) -> p t n", t=TILES)
        var, root, rstd, newton = (small[:, 64 + 8 * i:72 + 8 * i] for i in range(4))
        abs_sum = small[:, 96:102]
        scale, thresh, neg_thresh = small[:, 102:105], small[:, 105:108], small[:, 108:111]
        hid_scale = small[:, 111:112]
        warm = small[:, 112:120]
        den = small[:, 120:128].rearrange("p (r h) -> p r h", r=2)
        rden = small[:, 128:136].rearrange("p (r h) -> p r h", r=2)

        bank = ctx.enter_context(nc.psum_tensor("bank", [P, 8, 512], F32))
        ps_total = [bank[:, i, 0:1] for i in (2, 3, 0)]
        ps_xt = [bank[:, i, :] for i in (0, 1, 5, 6)]
        ps_up, ps_gate = bank[:, 2, :], bank[:, 3, :]
        ps_ffn = bank[:, 4:8:3, :].rearrange("p a (h n) -> p a h n", h=2)
        ps_proj, ps_score = bank[:, 0:2, :], bank[:, 2:4, :]
        ps_o, ps_tr, ps_sum, ps_y = bank[:, 4, :], bank[:, 5, :], bank[:, 6, :], bank[:, 7, :]

        x_loaded = [sem(f"x_loaded{b}") for b in range(B)]
        ident_loaded, consts_loaded = sem("ident_loaded"), sem("consts_loaded")
        t_loaded = [sem(f"t_loaded{w}") for w in range(3)]
        w_loaded = [sem(f"w_loaded{i}") for i in range(len(w_raw))]
        ln_step, root_done = sem("ln_step"), sem("root_done")
        xn_done, xn_done_pool = [sem(f"xn_done{b}") for b in range(B)], sem("xn_done_pool")
        abs_done, total_done, tern_step = sem("abs_done"), sem("total_done"), sem("tern_step")
        above, above_pool = sem("above"), sem("above_pool")
        tern_done = [sem(f"tern_done{w}") for w in range(3)]
        xt_done, xt_hi, xt_ready = sem("xt_done"), sem("xt_hi"), sem("xt_ready")
        flags_done = sem("flags_done")
        up_done = sem("up_done")
        tanh_done, gate_done, silu_done, hid_done = (sem(n) for n in ("tanh_done", "gate_done", "silu_done", "hid_done"))
        hid_hi, hid_ready, down_done = sem("hid_hi"), sem("hid_ready"), sem("down_done")
        ffn_added, w_hi = sem("ffn_added"), sem("w_hi")
        w_ready, w_ready_pool = sem("w_ready"), sem("w_ready_pool")

        inc_done, inc_read = sem("inc_done"), sem("inc_read")
        x_stat_loaded = [sem(f"x_stat_loaded{r}") for r in range(2)]
        zeroed = sem("zeroed")
        projected, proj_read = sem("projected"), sem("proj_read")
        rotated, clipped, exped = sem("rotated"), sem("clipped"), sem("exped")
        q_formed, den_done, rden_done, normed = (sem(n) for n in ("q_formed", "den_done", "rden_done", "normed"))
        k_formed, k_hi, k_ready = sem("k_formed"), sem("k_hi"), sem("k_ready")
        v_hi = sem("v_hi")
        transposed, tr_hi, tr_ready = sem("transposed"), sem("tr_hi"), sem("tr_ready")
        sum_done, sum_read = sem("sum_done"), sem("sum_read")
        scored, masked, p_hi, p_ready = sem("scored"), sem("masked"), sem("p_hi"), sem("p_ready")
        o_done, o_hi, o_copied, o_ready = sem("o_done"), sem("o_hi"), sem("o_copied"), sem("o_ready")
        state_hi, state_ready = sem("state_hi"), sem("state_ready")
        y_done, y_half, out_ready, out_stored = sem("y_done"), sem("y_half"), sem("out_ready"), sem("out_stored")

        block = ctx.enter_context(nc.Block())

        def normalize(engine, t, done):
            engine.tensor_scalar(xn[:, t], acc[:, t], moments[:, t, 0:1], rstd[:, t:t + 1],
                                 ALU.subtract, ALU.mult).then_inc(done, 1)

        def tern_half(region, w, half):
            if w == 2:
                at = T_DOWN + half * FF
                return region[:, at:at + FF]
            at = (T_UP, T_GATE)[w]
            return region[:, at:at + CT * FF].rearrange("p (c h n) -> p c h n", c=CT, h=2)[:, :, half]

        def compare_above(engine, w, half, done):
            engine.tensor_scalar(tern_half(tern, w, half), tern_half(t_raw, w, half), thresh[:, w:w + 1], None,
                                 ALU.is_gt).then_inc(done, 1)

        def w_chunk(s, i):
            return w_split[:, s, i * W_CHUNK:(i + 1) * W_CHUNK].rearrange("p (a n) -> p a n", a=2)

        def wait_weights(engine, chunks):
            on_pool = sum(i in W_ON_POOL for i in range(chunks))
            engine.wait_ge(w_ready, chunks - on_pool)
            if on_pool:
                engine.wait_ge(w_ready_pool, on_pool)

        def split_lo(engine, i, done):
            hi, lo = w_chunk(0, i), w_chunk(1, i)
            engine.wait_ge(w_hi, i + 1)
            engine.tensor_tensor(lo, w_raw[W_PLACE[i]], hi.bitcast(F32), ALU.subtract).then_inc(done, 1)

        def heads(ap):
            return ap.rearrange("p (h n) -> p h n", h=REP)

        def rope_a(what):
            return rope_k if what == "k" else rope_q[:, what % 2]

        def rope_b_place(what):
            return 0 if what == "k" else what % 2

        @block.sync
        def _(sp):
            x_in = x.rearrange("b (c p) n -> b p c n", p=P)
            out_v = out.rearrange("b (c p) n -> b p c n", p=P)
            n_const = 2 * NC * HD
            for b in range(B):
                sp.dma_start(acc[:, b * NC:(b + 1) * NC], x_in[b]).then_inc(x_loaded[b], 16)
            sp.dma_start(t_raw[:, T_UP:T_GATE], w_ffn[:, T_UP:T_GATE]).then_inc(t_loaded[0], 16)
            sp.dma_start(const_f[:, n_const:], consts[:, n_const:]).then_inc(ident_loaded, 16)
            sp.dma_start(t_raw[:, T_GATE:T_DOWN], w_ffn[:, T_GATE:T_DOWN]).then_inc(t_loaded[1], 16)
            sp.dma_start(t_raw[:, T_DOWN:], w_ffn[:, T_DOWN:]).then_inc(t_loaded[2], 16)
            sp.dma_start(const_f[:, 0:n_const], consts[:, 0:n_const]).then_inc(consts_loaded, 16)

            def load_weights(i):
                place = W_PLACE[i]
                if place in W_PLACE[:i]:
                    wait_weights(sp, max(j for j in range(i) if W_PLACE[j] == place) + 1)
                sp.dma_start(w_raw[place], w_attn[:, i * W_CHUNK:(i + 1) * W_CHUNK].rearrange("p (a n) -> p a n", a=2)
                             ).then_inc(w_loaded[place], 16)

            sp.wait_ge(xt_done, B * CT)
            for i in range(2):
                load_weights(i)
            for w in range(2):
                sp.wait_ge(tern_done[w], 2)
            for i in range(2, 4):
                load_weights(i)

            def load_x_stat(c, tile):
                r = tile % 2
                wait_round(sp, projected, c, 6 * 2, proj_index(tile - 2, 3) + 1)
                chunk = tile // B if c is None else c + tile // B
                sp.dma_start(x_stat[:, r].bitcast(F32),
                             xt_split[:, :, :, bass.ds(chunk * P + (tile % B) * S, P)].bitcast(F32)
                             ).then_inc(x_stat_loaded[r], 16)

            def store(c, tile):
                wait_round(sp, out_ready, c, 2, tile + 1, START)
                chunk = tile // B if c is None else c + tile // B
                b = tile % B
                sp.dma_start(out_v[b][:, bass.ds(chunk, 1), :],
                             acc[:, bass.ds(chunk + b * NC, 1), :]).then_inc(out_stored, 16)

            sp.wait_ge(xt_ready, B * CT)
            load_x_stat(None, 0)
            load_x_stat(None, 1)
            for i in range(4, W_CHUNKS):
                load_weights(i)
            with sp.Fori(0, ROUNDS) as c:
                for tile in range(2):
                    load_x_stat(c, tile + 2)
                    store(c, tile)
            for tile in range(TILES - 2, TILES):
                store(None, tile)
            sp.wait_ge(out_stored, 16 * TILES)

        @block.tensor
        def _(pe):
            for counter in (sum_done, inc_done, o_done, y_done):
                pe.sem_inc(counter, START)

            def total(w):
                pe.wait_ge(abs_done, 2 * w + 2)
                for i in range(2):
                    mm = nc.tensor.matmul(ps_total[w], ones_f, abs_sum[:, 2 * w + i:2 * w + i + 1],
                                          start=(i == 0), stop=(i == 1))
                mm.then_inc(total_done, 1)

            def transpose_xn(b):
                pe.wait_ge(xn_done[b], NC - b * XN_ON_POOL)
                if b:
                    pe.wait_ge(xn_done_pool, XN_ON_POOL)
                for half in range(CT):
                    for t in range(NC):
                        mm = nc.tensor.transpose(ps_xt[CT * b + half][:, t * P:(t + 1) * P],
                                                 xn[:, NC * b + t, half * P:(half + 1) * P], ident)
                    mm.then_inc(xt_done, 1)

            def hidden(step, ps, at):
                b, j = divmod(step, FT)
                for half in range(CT):
                    col = at + half * FF + j * P
                    for lo in range(2):
                        mm = nc.tensor.matmul(ps, tern[:, col:col + P], xt_split[:, lo, half, b * S:(b + 1) * S],
                                              start=(half == 0 and lo == 0), stop=(half == CT - 1 and lo == 1))
                return mm

            def up(step):
                if step < FT:
                    pe.wait_ge(tern_done[0], step // (FT // 2) + 1)
                pe.wait_ge(xt_ready, CT * (step // FT + 1))
                if step:
                    pe.wait_ge(silu_done, step)
                hidden(step, ps_up, T_UP).then_inc(up_done, 1)

            def gate(step):
                if step < FT:
                    pe.wait_ge(tern_done[1], step // (FT // 2) + 1)
                if step:
                    pe.wait_ge(hid_done, step)
                hidden(step, ps_gate, T_GATE).then_inc(gate_done, 1)

            def down(step):
                b, j = divmod(step, FT)
                if b == 0 and j % (FT // 2) == 0:
                    pe.wait_ge(tern_done[2], j // (FT // 2) + 1)
                if j == 0 and b:
                    pe.wait_ge(ffn_added, b)
                pe.wait_ge(hid_ready, b * FT + j + 1)
                for lo in range(2):
                    for t in range(NC):
                        mm = nc.tensor.matmul(ps_ffn[:, t // 2, t % 2], hid_split[:, lo, j % 2, t * P:(t + 1) * P],
                                              tern[:, T_DOWN + j * DM:T_DOWN + (j + 1) * DM],
                                              start=(j == 0 and lo == 0 and t % 2 == 0),
                                              stop=(j == FT - 1 and lo == 1), skip_group_check=True)
                mm.then_inc(down_done, 1)

            def project(c, tile, what):
                r = tile % 2
                n = proj_index(tile, what)
                if what == "k":
                    wait_round(pe, x_stat_loaded[r], c, 16, 16 * (tile // 2 + 1))
                wait_round(pe, proj_read, c, 12, n - 1)
                if what in ("k", "v"):
                    col = W_K if what == "k" else W_V
                    chunk = 0 if what == "k" else 1
                else:
                    col, chunk = W_Q + what * CT * KV, 2 + what
                if c is None and tile == 0:
                    wait_weights(pe, chunk + 1)
                passes = [(s, w, half) for half in range(CT) for s, w in ((0, 0), (0, 1), (1, 0))]
                for i, (s, w, half) in enumerate(passes):
                    at = col + half * KV
                    mm = nc.tensor.matmul(ps_proj[:, n % 2], x_stat[:, r, s, half],
                                          w_split[:, w, at:at + KV], start=(i == 0), stop=(i == len(passes) - 1))
                mm.then_inc(projected, 1)

            def transpose(c, tile, what):
                if what == "k":
                    wait_round(pe, k_formed, c, 2, tile + 1)
                    src = k_feat
                else:
                    wait_round(pe, normed, c, 8, KVH * tile + what + 1)
                    src = q_feat[:, what % 2]
                n = rope_index(tile, what)
                wait_round(pe, tr_ready, c, 10, n)
                for h in range(REP):
                    mm = nc.tensor.transpose(ps_tr[:, h * P:(h + 1) * P], src[:, h * P:(h + 1) * P], ident)
                mm.then_inc(transposed, 1)

            def slot(c, k):
                tile, g = tile_of(k), k % KVH
                r, kr = tile % 2, k % 2
                if is_unit(k):
                    wait_round(pe, tr_ready, c, 10, rope_index(tile, g) + 1)
                    wait_round(pe, masked, c, 8, k - 1, START)
                    for i, (s, m) in enumerate(((0, 0), (0, 1), (1, 0))):
                        mm = nc.tensor.matmul(ps_score[:, kr], kt_split[:, s, r, g * P:(g + 1) * P],
                                              qt_split[:, m, kr], start=(i == 0), stop=(i == 2))
                    mm.then_inc(scored, 1)
                projections = slot_projections(k)
                for t, what in projections[:1]:
                    project(c, t, what)
                if is_unit(k + 1):
                    transpose(c, tile_of(k + 1), (k + 1) % KVH)
                if k == 0:
                    for step in range(FFN_STEPS - DOWN_LAG, FFN_STEPS):
                        down(step)
                for t, what in projections[1:]:
                    project(c, t, what)
                if k == 0:
                    pe.wait_ge(ffn_added, B)
                    wait_weights(pe, W_CHUNKS)
                e = k - 2
                if is_unit(e):
                    wait_round(pe, o_hi, c, 8, e + 1)
                    tw, gw, pr = tile_of(e), e % KVH, e % 2
                    if gw == 0:
                        wait_round(pe, out_ready, c, 2, tw, START)
                    for s in range(2):
                        if s == 1:
                            wait_round(pe, o_ready, c, 8, e + 1, START)
                        for h in range(REP):
                            at = W_O + (gw * REP + h) * DM
                            first, last = gw == 0 and s == 0 and h == 0, gw == KVH - 1 and s == 1 and h == REP - 1
                            o_st = o_split[:, s, pr, h * P:(h + 1) * P]
                            if s == 0:
                                mm = nc.tensor.matmul(ps_y.rearrange("p (w n) -> p w n", w=2), o_st,
                                                      w_split[:, :, at:at + DM], start=first, stop=last)
                            else:
                                mm = nc.tensor.matmul(ps_y[:, 0:DM], o_st, w_split[:, 0, at:at + DM],
                                                      start=first, stop=last)
                    mm.then_inc(y_done, 1)
                if (g == 1 and 0 <= tile + 1 < TILES) or (g == 2 and has_state(tile + 1)):
                    new = tile + 1
                    wait_round(pe, k_ready, c, 2, new + 1)
                    wait_round(pe, sum_read, c, 4, 2 * new + g - 1, START)
                    if g == 1:
                        wait_round(pe, inc_read, c, 2, new - 1, START)
                    for s in range(2):
                        mm = nc.tensor.matmul(ps_sum, tri if g == 1 else ones, k_split[:, s, new % 2],
                                              start=(s == 0), stop=(s == 1))
                    mm.then_inc(sum_done, 1)
                if g == 3 and has_state(tile):
                    wait_round(pe, sum_read, c, 4, 2 * tile + 4, START)
                    wait_round(pe, proj_read, c, 12, proj_index(tile, "v") + 1)
                    for j in range(KVH):
                        cols = slice(j * P, (j + 1) * P)
                        for i, (s, m) in enumerate(((0, 0), (0, 1), (1, 0))):
                            mm = nc.tensor.matmul(ps_sum[:, cols], k_split[:, s, r, cols], v_split[:, m, r, cols],
                                                  start=(i == 0), stop=(i == 2))
                    mm.then_inc(inc_done, 1)
                if transposes_k(k):
                    transpose(c, tile + 1, "k")
                if is_unit(k):
                    wait_round(pe, o_copied, c, 8, k)
                    wait_round(pe, state_ready, c, 2, tile + 1)
                    with_state = c is not None or tile >= B
                    for i, (s, m) in enumerate(((0, 0), (0, 1), (1, 0)) if with_state else ()):
                        nc.tensor.matmul(ps_o, state_split[:, s, r, g * P:(g + 1) * P], qt_split[:, m, kr],
                                         start=(i == 0), stop=False)
                    wait_round(pe, proj_read, c, 12, proj_index(tile, "v") + 1)
                    wait_round(pe, p_hi, c, 8, k + 1)
                    for s in range(2):
                        nc.tensor.matmul(ps_o, v_split[:, s, r, g * P:(g + 1) * P], p_split[:, 0, kr],
                                         start=(s == 0 and not with_state), stop=False)
                    wait_round(pe, p_ready, c, 8, k + 1, START)
                    nc.tensor.matmul(ps_o, v_split[:, 0, r, g * P:(g + 1) * P], p_split[:, 1, kr],
                                     start=False, stop=True).then_inc(o_done, 1)

            pe.wait_ge(ident_loaded, 16)
            total(0)
            transpose_xn(0)
            transpose_xn(1)
            total(1)
            for step in range(FFN_STEPS):
                up(step)
                if step == 0:
                    total(2)
                gate(step)
                if step >= DOWN_LAG:
                    down(step - DOWN_LAG)
                if step in FILL_STEP:
                    if step == min(FILL_STEP):
                        pe.wait_ge(tern_step, 2 * 2 + 1)
                        pe.wait_ge(flags_done, 2)
                    slot(None, FILL_STEP[step])
            pe.wait_ge(silu_done, FFN_STEPS)
            for k in SLOTS_BEFORE:
                slot(None, k)
            with pe.Fori(0, ROUNDS) as c:
                for k in LOOP_SLOTS:
                    slot(c, k)
            for k in SLOTS_AFTER:
                slot(None, k)

        @block.vector
        def _(dve):
            v = nc.vector
            for counter in (masked, sum_read, inc_read, out_ready):
                dve.sem_inc(counter, START)
            step = [0]

            def chained(sem, ins):
                step[0] += 1
                ins.then_inc(sem, 1)
                dve.wait_ge(sem, step[0])

            for t in range(TILES):
                if t % NC == 0:
                    dve.wait_ge(x_loaded[t // NC], 16)
                ins = v.bn_stats(stats[:, t], acc[:, t])
            chained(ln_step, ins)
            for t in range(TILES):
                ins = v.bn_aggr(moments[:, t], stats[:, t])
            chained(ln_step, ins)
            chained(ln_step, v.tensor_scalar(var, moments[:, :, 1], LN_EPS, None, ALU.add))
            dve.wait_ge(root_done, 1)
            chained(ln_step, v.reciprocal(rstd, root))
            chained(ln_step, v.tensor_tensor(newton, rstd, rstd, ALU.mult))
            chained(ln_step, v.tensor_tensor(newton, newton, var, ALU.mult))
            chained(ln_step, v.tensor_scalar(newton, newton, -0.5, 1.5, ALU.mult, ALU.add))
            chained(ln_step, v.tensor_tensor(rstd, rstd, newton, ALU.mult))
            for t in range(TILES - XN_ON_POOL):
                normalize(v, t, xn_done[t // NC])

            step[0] = 0

            def threshold(w):
                one = slice(w, w + 1)
                dve.wait_ge(total_done, w + 1)
                chained(tern_step, v.tensor_scalar(scale[:, one], ps_total[w], SCALE_BLOCK, TERN_EPS,
                                                   ALU.mult, ALU.add))
                v.tensor_scalar(thresh[:, one], scale[:, one], 0.5, None, ALU.mult)
                chained(tern_step, v.tensor_scalar(neg_thresh[:, one], scale[:, one], -0.5, None, ALU.mult))

            compares = [0]

            def ternary(w, half):
                one = slice(w, w + 1)
                if (w, half) in ABOVE_ON_POOL:
                    dve.wait_ge(above_pool, ABOVE_ON_POOL.index((w, half)) + 1)
                else:
                    compares[0] += 1
                    compare_above(v, w, half, above)
                    dve.wait_ge(above, compares[0])
                dst = tern_half(tern, w, half)
                v.scalar_tensor_tensor(dst, tern_half(t_raw, w, half), neg_thresh[:, one], dst.bitcast(F32),
                                       ALU.is_lt, ALU.subtract).then_inc(tern_done[w], 1)

            def split_xt(b):
                for half in range(CT):
                    dve.wait_ge(xt_hi, b * CT + half + 1)
                    dst = xt_split[:, :, half, b * S:(b + 1) * S]
                    v.tensor_tensor(dst[:, 1], ps_xt[b * CT + half], dst[:, 0].bitcast(F32), ALU.subtract
                                    ).then_inc(xt_ready, 1)

            threshold(0)
            ternary(0, 0)
            threshold(1)
            split_xt(0)
            ternary(1, 0)
            threshold(2)
            chained(tern_step, v.tensor_tensor(hid_scale, scale[:, 1:2], scale[:, 2:3], ALU.mult))
            chained(tern_step, v.tensor_tensor(hid_scale, hid_scale, neg_thresh[:, 0:1], ALU.mult))

            def add_ffn(b):
                dve.wait_ge(down_done, (b + 1) * FT)
                for i in range(2):
                    half = acc[:, b * NC + 2 * i:b * NC + 2 * i + 2]
                    ins = v.tensor_tensor(half, ps_ffn[:, i], half, ALU.add)
                ins.then_inc(ffn_added, 1)

            def ffn_step(step):
                b, j = divmod(step, FT)
                dve.wait_ge(tanh_done, step + 1)
                v.scalar_tensor_tensor(hid[:, j % 2], hid[:, j % 2], 1.0, ps_up,
                                       ALU.add, ALU.mult).then_inc(silu_done, 1)
                dve.wait_ge(gate_done, step + 1)
                dve.wait_ge(silu_done, step + 1)
                v.scalar_tensor_tensor(hid[:, j % 2], ps_gate, hid_scale, hid[:, j % 2],
                                       ALU.mult, ALU.mult).then_inc(hid_done, 1)
                if step == FT + DOWN_LAG - 1:
                    add_ffn(0)
                if step in TERN_STEP:
                    ternary(*TERN_STEP[step])
                if step == XT_STEP:
                    split_xt(1)
                if step in W_STEP and W_STEP[step] not in W_ON_POOL:
                    split_lo(v, W_STEP[step], w_ready)

            def rotate(c, tile, what):
                n = proj_index(tile, what)
                chunk = tile // B if c is None else c + tile // B
                wait_round(dve, projected, c, 12, n + 1)
                src = ps_proj[:, n % 2]
                v.tensor_tensor(heads(rope_a(what)), heads(src),
                                cos_t[:, bass.ds(chunk, 1), :].broadcast_to([P, REP, HD]), ALU.mult)
                swapped = src.rearrange("p (h u e) -> p h u e", h=REP, u=2)[:, :, ::-1, :]
                sin = sin_t[:, bass.ds(chunk, 1), :].rearrange("p o (u e) -> p o u e", u=2)
                if what == 0:
                    wait_round(dve, rotated, c, 10, rope_index(tile, "k") + 1)
                v.tensor_tensor(rope_b[:, rope_b_place(what)].rearrange("p (h u e) -> p h u e", h=REP, u=2), swapped,
                                sin.broadcast_to([P, REP, 2, HD // 2]), ALU.mult).then_inc(proj_read, 1)

            def split_transposed(c, tile, what):
                w = rope_index(tile, what)
                wait_round(dve, tr_hi, c, 10, w + 1)
                dst = kt_split[:, :, tile % 2] if what == "k" else qt_split[:, :, what % 2]
                v.tensor_tensor(dst[:, 1], ps_tr, dst[:, 0].bitcast(F32), ALU.subtract).then_inc(tr_ready, 1)

            def slot(c, k):
                tile, g = tile_of(k), k % KVH
                new = tile + 1
                if g == 1 and 0 <= new < TILES:
                    wait_round(dve, exped, c, 10, rope_index(new, "k") + 1)
                    v.scalar_tensor_tensor(k_feat, rope_k, 1.0, k_feat,
                                           ALU.add, ALU.max).then_inc(k_formed, 1)
                f = k + 2
                if is_unit(f):
                    ft, fg, fr = tile_of(f), f % KVH, f % 2
                    wait_round(dve, exped, c, 10, rope_index(ft, fg) + 1)
                    v.scalar_tensor_tensor(q_feat[:, fr], rope_q[:, fr], 1.0, q_feat[:, fr],
                                           ALU.add, ALU.max).then_inc(q_formed, 1)
                if is_unit(k):
                    wait_round(dve, scored, c, 8, k + 1)
                    wait_round(dve, p_ready, c, 8, k - 1, START)
                    v.tensor_tensor(heads(p_mask[:, k % 2]), heads(ps_score[:, k % 2]),
                                    mask.rearrange("p (o n) -> p o n", o=1).broadcast_to([P, REP, P]),
                                    ALU.mult).then_inc(masked, 1)
                if g == 2 and 0 <= tile - 1 < TILES:
                    old = tile - 1
                    wait_round(dve, y_done, c, 8, KVH * old + KVH, START)
                    chunk = old // B if c is None else c + old // B
                    dst = acc[:, bass.ds(chunk + (old % B) * NC, 1), :]
                    y = ps_y.rearrange("p (w n) -> p w n", w=2)
                    v.tensor_tensor(dst, y[:, 0:1], dst, ALU.add).then_inc(y_half, 1)
                    wait_round(dve, y_half, c, 2, old + 1)
                    v.tensor_tensor(dst, y[:, 1:2], dst, ALU.add).then_inc(out_ready, 1)
                if g == 1 and 0 <= new < TILES:
                    wait_round(dve, k_hi, c, 2, new + 1)
                    v.tensor_tensor(k_split[:, 1, new % 2], k_feat, k_split[:, 0, new % 2].bitcast(F32),
                                    ALU.subtract).then_inc(k_ready, 1)
                if is_unit(f):
                    wait_round(dve, q_formed, c, 8, f + 1)
                    wait_round(dve, sum_read, c, 4, 2 * ft + 1, START)
                    wait_round(dve, normed, c, 8, f - 1)
                    wait_round(dve, rotated, c, 10, rope_index(*divmod(min(f + 1, UNITS - 1), KVH)) + 1)
                    for h in range(REP):
                        cols = slice(h * P, (h + 1) * P)
                        ins = v.tensor_tensor_reduce(out=rope_b[:, (fr + 1) % 2, cols], in0=q_feat[:, fr, cols],
                                                     in1=z_sum[ft % 2][:, fg * P:(fg + 1) * P], scale=1.0,
                                                     scalar=DEN_EPS, op0=ALU.mult, op1=ALU.add,
                                                     accum_out=den[:, fr, h:h + 1])
                    ins.then_inc(den_done, 1)
                if k == 0:
                    add_ffn(B - 1)
                def reciprocal():
                    if is_unit(f):
                        wait_round(dve, den_done, c, 8, f + 1)
                        v.reciprocal(rden[:, fr], den[:, fr]).then_inc(rden_done, 1)

                def split_q():
                    if is_unit(k + 1):
                        split_transposed(c, tile_of(k + 1), (k + 1) % KVH)

                projections = slot_projections(k)
                if len(projections) < 2:
                    split_q()
                    reciprocal()
                for i, (t, what) in enumerate(projections):
                    if what == "v":
                        wait_round(dve, v_hi, c, 2, t + 1)
                        v.tensor_tensor(v_split[:, 1, t % 2], ps_proj[:, proj_index(t, what) % 2],
                                        v_split[:, 0, t % 2].bitcast(F32), ALU.subtract).then_inc(proj_read, 1)
                    else:
                        rotate(c, t, what)
                    if i == 0 and len(projections) == 2:
                        reciprocal()
                        split_q()
                if g == 1 and 0 <= new < TILES:
                    wait_round(dve, sum_done, c, 4, 2 * new + 1, START)
                    wait_round(dve, sum_read, c, 4, 2 * new - 2, START)
                    v.tensor_tensor(z_sum[new % 2], ps_sum, k_total[:, new % 2], ALU.add).then_inc(sum_read, 1)
                if g == 2 and has_state(new):
                    wait_round(dve, sum_done, c, 4, 2 * new + 2, START)
                    v.tensor_tensor(k_total[:, new % 2], ps_sum, k_total[:, new % 2], ALU.add
                                    ).then_inc(sum_read, 1)
                if transposes_k(k):
                    split_transposed(c, new, "k")
                if g == 3 and has_state(tile):
                    wait_round(dve, inc_done, c, 2, tile + 1, START)
                    wait_round(dve, state_ready, c, 2, tile + 1)
                    v.tensor_tensor(state[tile % 2], ps_sum, state[tile % 2], ALU.add).then_inc(inc_read, 1)
            for step in range(FFN_STEPS):
                ffn_step(step)
                if step in FILL_STEP:
                    if step == min(FILL_STEP):
                        dve.wait_ge(consts_loaded, 16)
                        dve.wait_ge(zeroed, 2)
                    if FILL_STEP[step] == -4:
                        wait_weights(dve, 4)
                    slot(None, FILL_STEP[step])
            wait_weights(dve, W_CHUNKS)
            for k in SLOTS_BEFORE:
                slot(None, k)
            with dve.Fori(0, ROUNDS) as c:
                for k in LOOP_SLOTS:
                    slot(c, k)
            for k in SLOTS_AFTER:
                slot(None, k)

        @block.scalar
        def _(act):
            s = nc.scalar
            act.wait_ge(ln_step, 3)
            s.activation(root, var, ACT.Sqrt).then_inc(root_done, 1)

            def abs_sums(w):
                act.wait_ge(t_loaded[w], 16)
                for i in range(2 * w, 2 * w + 2):
                    if i:
                        act.wait_ge(abs_done, i)
                    s.activation(hid, t_raw[:, i * FF:(i + 1) * FF].rearrange("p (r n) -> p r n", r=2), ACT.Abs,
                                 accum_out=abs_sum[:, i:i + 1]).then_inc(abs_done, 1)

            def xt_hi_of(b):
                for half in range(CT):
                    act.wait_ge(xt_done, b * CT + half + 1)
                    s.activation(xt_split[:, 0, half, b * S:(b + 1) * S], ps_xt[b * CT + half],
                                 ACT.Copy).then_inc(xt_hi, 1)

            abs_sums(0)
            s.activation(warm, var, ACT.Tanh)
            abs_sums(1)
            xt_hi_of(0)
            abs_sums(2)
            xt_hi_of(1)
            s.activation(tri, mask, ACT.Copy).then_inc(flags_done, 1)
            s.activation(ones, ones_f, ACT.Copy).then_inc(flags_done, 1)
            act.wait_ge(abs_done, 6)
            act.wait_ge(tern_step, 2)

            def ffn_step(step):
                b, j = divmod(step, FT)
                act.wait_ge(up_done, step + 1)
                if step >= 2:
                    act.wait_ge(hid_ready, step - 1)
                s.activation(hid[:, j % 2], ps_up, ACT.Tanh, scale=neg_thresh[:, 0:1]).then_inc(tanh_done, 1)
                if step in W_STEP:
                    i = W_STEP[step]
                    act.wait_ge(w_loaded[W_PLACE[i]], 16 * W_PLACE[:i + 1].count(W_PLACE[i]))
                    s.activation(w_chunk(0, i), w_raw[W_PLACE[i]], ACT.Copy).then_inc(w_hi, 1)
                act.wait_ge(hid_done, step + 1)
                if step >= 2:
                    act.wait_ge(down_done, step - 1)
                s.activation(hid_split[:, 0, j % 2], hid[:, j % 2], ACT.Copy).then_inc(hid_hi, 1)

            def exp(c, tile, what):
                w = rope_index(tile, what)
                wait_round(act, rotated, c, 10, w + 1)
                if what == "k":
                    wait_round(act, transposed, c, 10, rope_index(tile - 1, "k") + 1)
                    wait_round(act, k_ready, c, 2, tile)
                    dst = k_feat
                else:
                    wait_round(act, transposed, c, 10, rope_index(*divmod(KVH * tile + what - 2, KVH)) + 1)
                    dst = q_feat[:, what % 2]
                s.activation(dst, rope_a(what), ACT.Relu, scale=-1.0).then_inc(clipped, 1)
                wait_round(act, clipped, c, 10, w + 1)
                s.activation(dst, dst, ACT.Exp, scale=-1.0).then_inc(exped, 1)

            def split_transposed(c, tile, what):
                wait_round(act, transposed, c, 10, rope_index(tile, what) + 1)
                if what == "k":
                    wait_round(act, o_done, c, 8, KVH * (tile - 1), START)
                    dst = kt_split[:, 0, tile % 2]
                else:
                    wait_round(act, o_done, c, 8, KVH * tile + what - 1, START)
                    dst = qt_split[:, 0, what % 2]
                s.activation(dst, ps_tr, ACT.Copy).then_inc(tr_hi, 1)

            def slot(c, k):
                tile, g = tile_of(k), k % KVH
                new = tile + 1
                if is_unit(k - 1):
                    wait_round(act, o_done, c, 8, k, START)
                    wait_round(act, y_done, c, 8, k - 2, START)
                    s.activation(o_split[:, 0, (k - 1) % 2], ps_o, ACT.Copy).then_inc(o_hi, 1)
                    wait_round(act, o_ready, c, 8, k - 1, START)
                    s.activation(o_copy[:, (k - 1) % 2], ps_o, ACT.Copy).then_inc(o_copied, 1)
                if g == 1 and 0 <= new < TILES:
                    wait_round(act, k_formed, c, 2, new + 1)
                    wait_round(act, inc_done, c, 2, new - 1, START)
                    s.activation(k_split[:, 0, new % 2], k_feat, ACT.Copy).then_inc(k_hi, 1)
                if is_unit(k):
                    if k == 0:
                        act.wait_ge(down_done, FFN_STEPS)
                    wait_round(act, masked, c, 8, k + 1, START)
                    wait_round(act, o_done, c, 8, k - 1, START)
                    s.activation(p_split[:, 0, k % 2], p_mask[:, k % 2], ACT.Copy).then_inc(p_hi, 1)
                if g == 0 and 0 <= new < TILES:
                    wait_round(act, projected, c, 12, proj_index(new, "v") + 1)
                    wait_round(act, o_done, c, 8, KVH * (new - 1), START)
                    s.activation(v_split[:, 0, new % 2], ps_proj[:, proj_index(new, "v") % 2], ACT.Copy
                                 ).then_inc(v_hi, 1)
                if is_unit(k + 1):
                    split_transposed(c, tile_of(k + 1), (k + 1) % KVH)
                if transposes_k(k):
                    split_transposed(c, new, "k")
                for t, what in slot_rotations(k - 1):
                    exp(c, t, what)
                if g == 0 and splits_state(tile - 1):
                    old = tile - 1
                    if old < 0 and c is None:
                        act.wait_ge(zeroed, old + B + 2)
                    wait_round(act, inc_read, c, 2, old + 1, START)
                    wait_round(act, o_done, c, 8, KVH * (old + 1), START)
                    s.activation(state_split[:, 0, old % 2], state[old % 2], ACT.Copy).then_inc(state_hi, 1)

            for step in range(FFN_STEPS):
                ffn_step(step)
                if step in FILL_STEP:
                    if FILL_STEP[step] == -3:
                        wait_weights(act, 7)
                    slot(None, FILL_STEP[step])
            for k in SLOTS_BEFORE:
                slot(None, k)
            with act.Fori(0, ROUNDS) as c:
                for k in LOOP_SLOTS:
                    slot(c, k)
            for k in SLOTS_AFTER:
                slot(None, k)

        @block.gpsimd
        def _(pool):
            p = nc.gpsimd
            for counter in (p_ready, o_ready):
                pool.sem_inc(counter, START)

            pool.wait_ge(ln_step, LN_STEPS)
            for t in range(TILES - XN_ON_POOL, TILES):
                normalize(p, t, xn_done_pool)
            for w, half in ABOVE_ON_POOL:
                pool.wait_ge(tern_step, 2 * w + 2)
                compare_above(p, w, half, above_pool)

            def ffn_step(step):
                j = step % FT
                pool.wait_ge(hid_hi, step + 1)
                p.tensor_tensor(hid_split[:, 1, j % 2], hid[:, j % 2], hid_split[:, 0, j % 2].bitcast(F32),
                                ALU.subtract).then_inc(hid_ready, 1)
                if step in W_STEP and W_STEP[step] in W_ON_POOL:
                    split_lo(p, W_STEP[step], w_ready_pool)
                if step == min(FILL_STEP) - 1:
                    for w in range(3):
                        pool.wait_ge(tern_done[w], 2)
                    p.memset(k_total, 0.0).then_inc(zeroed, 1)
                    p.memset(state[0], 0.0).then_inc(zeroed, 1)

            def slot(c, k):
                tile, g = tile_of(k), k % KVH
                new = tile + 1
                if is_unit(k - 1):
                    r = (k - 1) % 2
                    wait_round(pool, o_copied, c, 8, k)
                    p.tensor_tensor(o_split[:, 1, r], o_copy[:, r], o_split[:, 0, r].bitcast(F32), ALU.subtract
                                    ).then_inc(o_ready, 1)
                if is_unit(k):
                    wait_round(pool, p_hi, c, 8, k + 1)
                    p.tensor_tensor(p_split[:, 1, k % 2], p_mask[:, k % 2], p_split[:, 0, k % 2].bitcast(F32),
                                    ALU.subtract).then_inc(p_ready, 1)
                f = k + 2
                if is_unit(f):
                    wait_round(pool, rden_done, c, 8, f + 1)
                    d = rden[:, f % 2].rearrange("p (h o) -> p h o", o=1).broadcast_to([P, REP, P])
                    p.tensor_tensor(heads(q_feat[:, f % 2]), heads(q_feat[:, f % 2]), d, ALU.mult
                                    ).then_inc(normed, 1)
                if g == 2 and splits_state(tile - 1):
                    old = tile - 1
                    wait_round(pool, state_hi, c, 2, old + B + 1)
                    p.tensor_tensor(state_split[:, 1, old % 2], state[old % 2],
                                    state_split[:, 0, old % 2].bitcast(F32), ALU.subtract).then_inc(state_ready, 1)
                for t, what in slot_rotations(k):
                    wait_round(pool, proj_read, c, 12, proj_index(t, what) + 1)
                    p.tensor_tensor(rope_a(what), rope_a(what), rope_b[:, rope_b_place(what)], ALU.add
                                    ).then_inc(rotated, 1)

            for step in range(FFN_STEPS):
                ffn_step(step)
                if step in FILL_STEP:
                    slot(None, FILL_STEP[step])
            wait_weights(pool, W_CHUNKS)
            p.memset(state[1], 0.0).then_inc(zeroed, 1)
            for k in SLOTS_BEFORE:
                slot(None, k)
            with pool.Fori(0, ROUNDS) as c:
                for k in LOOP_SLOTS:
                    slot(c, k)
            for k in SLOTS_AFTER:
                slot(None, k)


def constants():
    inv_freq = (1.0 / np.float32(10000.0) ** (np.arange(0, HD, 2, dtype=np.float32) / np.float32(HD)))
    freqs = np.outer(np.arange(S, dtype=np.float32), inv_freq.astype(np.float32)).astype(np.float32)
    cos = np.concatenate([np.cos(freqs)] * 2, -1).reshape(NC, P, HD).transpose(1, 0, 2).reshape(P, -1)
    sin = np.concatenate([-np.sin(freqs), np.sin(freqs)], -1).reshape(NC, P, HD).transpose(1, 0, 2).reshape(P, -1)
    mask = np.triu(np.ones((P, P)))
    return np.concatenate([cos, sin, mask, np.eye(P), np.ones((P, P))], 1).astype(np.float32)


def kernel(L0_attn_x, L0_attn_Wq, L0_attn_Wk, L0_attn_Wv, L0_attn_Wo, L0_ffn_W_up, L0_ffn_W_gate, L0_ffn_W_down):
    import concourse.bacc as bacc
    from concourse.bass_utils import run_bass_kernel_spmd

    def columns(w):
        w = np.asarray(w)
        return w.T.reshape(-1, P, w.shape[0]).transpose(1, 0, 2).reshape(P, -1)

    arrays = {
        "x": np.ascontiguousarray(np.asarray(L0_attn_x)),
        "w_attn": np.ascontiguousarray(np.concatenate(
            [columns(w) for w in (L0_attn_Wk, L0_attn_Wv, *np.split(np.asarray(L0_attn_Wq), KVH), L0_attn_Wo)], 1)),
        "w_ffn": np.ascontiguousarray(np.concatenate(
            [columns(w) for w in (L0_ffn_W_up, L0_ffn_W_gate, L0_ffn_W_down)], 1)),
        "consts": constants(),
    }
    nc = bacc.Bacc("TRN2", target_bir_lowering=False, num_devices=1)
    args = [nc.dram_tensor(n, a.shape, F32, kind="ExternalInput").ap() for n, a in arrays.items()]
    out = nc.dram_tensor("out", (B, S, DM), F32, kind="ExternalOutput").ap()
    build(nc, *args, out)
    r = run_bass_kernel_spmd(nc, [arrays], core_ids=[0])
    return r.results[0]["out"]
```
